# Optimizing a Trainium2 kernel written in Bass

```python
import numpy as np
import jax
import jax.numpy as jnp

def _softmax(x, axis=-1):
    return jax.nn.softmax(x, axis=axis)

def _gelu(x):
    return jax.nn.gelu(x, approximate=True)

def _silu(x):
    return jax.nn.silu(x)

def _sigmoid(x):
    return jax.nn.sigmoid(x)

def _layernorm(x, axis=-1, eps=1e-05):
    m = jnp.mean(x, axis=axis, keepdims=True)
    v = jnp.var(x, axis=axis, keepdims=True)
    return (x - m) / jnp.sqrt(v + eps)

def _scatter_add(tgt, idx, src, axis=0):
    return tgt.at[idx].add(src)

def _segment_sum(src, seg, n):
    return jax.ops.segment_sum(src, seg, n)
kernel_name = 'mk_adj_resnorm_d4_adj_r2_8c9fa1'

def setup_inputs(seed: int=0):
    np.random.seed(seed)
    _w = jnp.asarray

    def _rec_inputs():
        import jax
        import jax.numpy as jnp
        _gk = jax.random.key(seed)
        x = 7.22e-05 + 1 * jax.random.normal(jax.random.fold_in(_gk, 1), (16, 512, 256), jnp.float32)
        _a = jax.random.bernoulli(jax.random.fold_in(_gk, 2), 0.03125, (16, 512, 512))
        adj = _a.astype(jnp.int32)
        return (x, adj)
    x, adj = _rec_inputs()

    def _L0_gnn_setup():
        import jax, jax.numpy as jnp
        import numpy as np
        NEG_INF = -1000000000.0
        ALPHA = 0.1
        key = jax.random.key(seed)
        k1, k2, k3, k4, k5 = jax.random.split(key, 5)
        B, N, Din, Dout = (8, 1024, 256, 256)
        features = jax.random.normal(k1, (B, N, Din), dtype=jnp.float32)
        graph = jax.random.randint(k2, (B, N, N), 0, 2, dtype=jnp.int64)
        lim_w = 1.414 * np.sqrt(6.0 / (Din + Dout))
        w = jax.random.uniform(k3, (Din, Dout), jnp.float32, -lim_w, lim_w)
        lim_a = 1.414 * np.sqrt(6.0 / (Dout + 1))
        a1 = jax.random.uniform(k4, (Dout, 1), jnp.float32, -lim_a, lim_a)
        a2 = jax.random.uniform(k5, (Dout, 1), jnp.float32, -lim_a, lim_a)
        return {'features': features, 'graph': graph, 'w': w, 'a1': a1, 'a2': a2}
    _L0_gnn_all = _L0_gnn_setup()
    _L0_gnn_in = {k: v for k, v in _L0_gnn_all.items() if k in ('w', 'a1', 'a2')}
    del _L0_gnn_all

    def _L1_gnn_setup():
        import jax, jax.numpy as jnp
        import numpy as np
        L = 3
        D = 256
        B, N = (8, 512)
        EPS = 1e-05

        def layernorm(x, gamma, beta):
            mu = jnp.mean(x, axis=-1, keepdims=True)
            var = jnp.var(x, axis=-1, keepdims=True)
            return (x - mu) * jax.lax.rsqrt(var + EPS) * gamma + beta
        key = jax.random.key(seed)
        ks = jax.random.split(key, 12)
        s = 1.0 / np.sqrt(D)
        node_features = jax.random.normal(ks[0], (B, N, D), dtype=jnp.float32)
        adjacency_matrix = jax.random.randint(ks[1], (B, N, N), 0, 2, dtype=jnp.int32)
        return {'node_features': node_features, 'adjacency_matrix': adjacency_matrix, 'attn_w': jax.random.normal(ks[2], (L, 2 * D), dtype=jnp.float32) * (1.0 / np.sqrt(2 * D)), 'attn_b': jax.random.normal(ks[3], (L,), dtype=jnp.float32) * 0.01, 'W1': jax.random.normal(ks[4], (L, D, 4 * D), dtype=jnp.float32) * s, 'b1': jnp.zeros((L, 4 * D), dtype=jnp.float32), 'W2': jax.random.normal(ks[5], (L, 4 * D, D), dtype=jnp.float32) * (1.0 / np.sqrt(4 * D)), 'b2': jnp.zeros((L, D), dtype=jnp.float32), 'g1': jnp.ones((L, D), dtype=jnp.float32), 'beta1': jnp.zeros((L, D), dtype=jnp.float32), 'g2': jnp.ones((L, D), dtype=jnp.float32), 'beta2': jnp.zeros((L, D), dtype=jnp.float32)}
    _L1_gnn_all = _L1_gnn_setup()
    _L1_gnn_in = {k: v for k, v in _L1_gnn_all.items() if k in ('attn_w', 'attn_b', 'W1', 'b1', 'W2', 'b2', 'g1', 'beta1', 'g2', 'beta2')}
    del _L1_gnn_all

    def _L2_gnn_setup():
        import jax, jax.numpy as jnp
        import numpy as np
        ALPHA = 0.2
        K_NUM = 16
        NEG_INF = -9000000000000000.0
        key = jax.random.key(seed)
        k1, k2, k3, k4 = jax.random.split(key, 4)
        B, N, F_in, F_out = (4, 1024, 256, 256)
        h = jax.random.normal(k1, (B, N, F_in), dtype=jnp.float32)
        adj = jax.random.randint(k2, (B, N, N), 0, 2, dtype=jnp.int32)

        def xavier(k, shape, gain=1.414):
            fan_in, fan_out = (shape[0], shape[1])
            bound = gain * np.sqrt(6.0 / (fan_in + fan_out))
            return jax.random.uniform(k, shape, jnp.float32, -bound, bound)
        W = xavier(k3, (F_in, F_out))
        a = xavier(k4, (2 * F_out, 1))
        return {'h': h, 'adj': adj, 'W': W, 'a': a}
    _L2_gnn_all = _L2_gnn_setup()
    _L2_gnn_in = {k: v for k, v in _L2_gnn_all.items() if k in ('W', 'a')}
    del _L2_gnn_all

    def _L3_gnn_setup():
        import jax, jax.numpy as jnp
        import numpy as np
        B, N, D = (8, 512, 256)
        NH = 8
        DK = D // NH
        key = jax.random.key(seed)
        ks = jax.random.split(key, 6)
        x = jax.random.normal(ks[0], (B, N, D), dtype=jnp.float32)
        adj = jax.random.randint(ks[1], (B, N, N), 0, 2, dtype=jnp.int32)
        adj = jnp.maximum(adj, jnp.eye(N, dtype=jnp.int32)[None])
        s = 1.0 / np.sqrt(D)
        Wq = jax.random.normal(ks[2], (D, D), dtype=jnp.float32) * s
        Wk = jax.random.normal(ks[3], (D, D), dtype=jnp.float32) * s
        Wv = jax.random.normal(ks[4], (D, D), dtype=jnp.float32) * s
        Wo = jax.random.normal(ks[5], (D, D), dtype=jnp.float32) * s
        return {'x': x, 'adj': adj, 'Wq': Wq, 'Wk': Wk, 'Wv': Wv, 'Wo': Wo}
    _L3_gnn_all = _L3_gnn_setup()
    _L3_gnn_in = {k: v for k, v in _L3_gnn_all.items() if k in ('Wq', 'Wk', 'Wv', 'Wo')}
    del _L3_gnn_all
    return {'x': x, 'adj': adj, 'L0_gnn_w': _L0_gnn_in['w'], 'L0_gnn_a1': _L0_gnn_in['a1'], 'L0_gnn_a2': _L0_gnn_in['a2'], 'L1_gnn_attn_w': _L1_gnn_in['attn_w'], 'L1_gnn_attn_b': _L1_gnn_in['attn_b'], 'L1_gnn_W1': _L1_gnn_in['W1'], 'L1_gnn_b1': _L1_gnn_in['b1'], 'L1_gnn_W2': _L1_gnn_in['W2'], 'L1_gnn_b2': _L1_gnn_in['b2'], 'L1_gnn_g1': _L1_gnn_in['g1'], 'L1_gnn_beta1': _L1_gnn_in['beta1'], 'L1_gnn_g2': _L1_gnn_in['g2'], 'L1_gnn_beta2': _L1_gnn_in['beta2'], 'L2_gnn_W': _L2_gnn_in['W'], 'L2_gnn_a': _L2_gnn_in['a'], 'L3_gnn_Wq': _L3_gnn_in['Wq'], 'L3_gnn_Wk': _L3_gnn_in['Wk'], 'L3_gnn_Wv': _L3_gnn_in['Wv'], 'L3_gnn_Wo': _L3_gnn_in['Wo']}

def reference(x, adj, L0_gnn_w, L0_gnn_a1, L0_gnn_a2, L1_gnn_attn_w, L1_gnn_attn_b, L1_gnn_W1, L1_gnn_b1, L1_gnn_W2, L1_gnn_b2, L1_gnn_g1, L1_gnn_beta1, L1_gnn_g2, L1_gnn_beta2, L2_gnn_W, L2_gnn_a, L3_gnn_Wq, L3_gnn_Wk, L3_gnn_Wv, L3_gnn_Wo):
    import jax
    import jax.numpy as jnp

    def _L0_gnn_ref(features, graph, w, a1, a2):
        import jax, jax.numpy as jnp
        import numpy as np
        NEG_INF = -1000000000.0
        ALPHA = 0.1
        hidden = jnp.einsum('bni,io->bno', features, w)
        s1 = hidden @ a1
        s2 = hidden @ a2
        e = jax.nn.leaky_relu(s1 + jnp.swapaxes(s2, 1, 2), negative_slope=ALPHA)
        e = jnp.where(graph == 0, NEG_INF, e)
        attn = jax.nn.softmax(e, axis=-1)
        h_prime = jnp.einsum('bij,bjo->bio', attn, hidden)
        return jax.nn.elu(h_prime)

    def _L1_gnn_ref(node_features, adjacency_matrix, attn_w, attn_b, W1, b1, W2, b2, g1, beta1, g2, beta2):
        import jax, jax.numpy as jnp
        import numpy as np
        L = 3
        D = 256
        B, N = (8, 512)
        EPS = 1e-05

        def layernorm(x, gamma, beta):
            mu = jnp.mean(x, axis=-1, keepdims=True)
            var = jnp.var(x, axis=-1, keepdims=True)
            return (x - mu) * jax.lax.rsqrt(var + EPS) * gamma + beta
        n = adjacency_matrix.shape[-1]
        mask = adjacency_matrix.astype(jnp.float32) + jnp.eye(n, dtype=jnp.float32) > 0
        x = node_features
        d = x.shape[-1]
        for l in range(attn_w.shape[0]):
            si = x @ attn_w[l, :d]
            sj = x @ attn_w[l, d:]
            scores = si[:, :, None] + sj[:, None, :] + attn_b[l]
            scores = jnp.where(scores >= 0, scores, 0.2 * scores)
            scores = jnp.where(mask, scores, -jnp.inf)
            attn = jax.nn.softmax(scores, axis=-1)
            agg = jnp.einsum('bij,bjd->bid', attn, x)
            h = layernorm(x + agg, g1[l], beta1[l])
            ff = jax.nn.gelu(h @ W1[l] + b1[l], approximate=False) @ W2[l] + b2[l]
            x = layernorm(h + ff, g2[l], beta2[l])
        return x

    def _L2_gnn_ref(h, adj, W, a):
        import jax, jax.numpy as jnp
        import numpy as np
        ALPHA = 0.2
        K_NUM = 16
        NEG_INF = -9000000000000000.0
        F_out = W.shape[1]
        Wh = jnp.einsum('bnf,fo->bno', h, W)
        a1, a2 = (a[:F_out, 0], a[F_out:, 0])
        e_src = Wh @ a1
        e_dst = Wh @ a2
        e = e_src[:, :, None] + e_dst[:, None, :]
        e = jnp.where(e > 0, e, ALPHA * e)
        e = jnp.where(adj > 0, e, NEG_INF)
        attention = jax.nn.softmax(e, axis=2)
        topk_vals = jax.lax.top_k(attention, K_NUM)[0]
        kth = topk_vals[:, :, -1:]
        attention = jnp.where(attention < kth, 0.0, attention)
        h_prime = jnp.einsum('bij,bjo->bio', attention, Wh)
        return jax.nn.elu(h_prime)

    def _L3_gnn_ref(x, adj, Wq, Wk, Wv, Wo):
        import jax, jax.numpy as jnp
        import numpy as np
        B, N, D = (8, 512, 256)
        NH = 8
        DK = D // NH
        b, n, d = x.shape
        sqrt_dk = jnp.asarray(np.sqrt(DK), dtype=x.dtype)

        def heads(t):
            return t.reshape(b, n, NH, DK).transpose(0, 2, 1, 3)
        q = heads(x @ Wq)
        k = heads(x @ Wk)
        v = heads(x @ Wv)
        scores = jnp.einsum('bhnd,bhmd->bhnm', q, k) / sqrt_dk
        mask = adj.astype(bool)[:, None]
        scores = jnp.where(mask, scores, -jnp.inf)
        attn = jax.nn.softmax(scores, axis=-1)
        out = jnp.einsum('bhnm,bhmd->bhnd', attn, v)
        out = out.transpose(0, 2, 1, 3).reshape(b, n, d)
        return jax.nn.relu(out) @ Wo
    x = _layernorm(x + _L0_gnn_ref(x, adj, L0_gnn_w, L0_gnn_a1, L0_gnn_a2), axis=-1)
    x = _layernorm(x + _L1_gnn_ref(x, adj, L1_gnn_attn_w, L1_gnn_attn_b, L1_gnn_W1, L1_gnn_b1, L1_gnn_W2, L1_gnn_b2, L1_gnn_g1, L1_gnn_beta1, L1_gnn_g2, L1_gnn_beta2), axis=-1)
    x = _layernorm(x + _L2_gnn_ref(x, adj, L2_gnn_W, L2_gnn_a), axis=-1)
    x = _layernorm(x + _L3_gnn_ref(x, adj, L3_gnn_Wq, L3_gnn_Wk, L3_gnn_Wv, L3_gnn_Wo), axis=-1)
    return x

_drawn_inputs = setup_inputs


def setup_inputs(seed=0):
    import zlib

    import numpy as np

    out = dict(_drawn_inputs(seed))
    spreads = {'L1_gnn_b1': (0.0, 0.1),
     'L1_gnn_b2': (0.0, 0.1),
     'L1_gnn_g1': (1.0, 0.2),
     'L1_gnn_beta1': (0.0, 0.1),
     'L1_gnn_g2': (1.0, 0.2),
     'L1_gnn_beta2': (0.0, 0.1)}
    factors = {'L1_gnn_attn_b': 64.0}
    for name, (base, spread) in spreads.items():
        noise = np.random.default_rng([zlib.crc32(name.encode()), seed]).standard_normal(out[name].shape)
        drawn = base * np.exp(spread * noise) if base else spread * noise
        out[name] = jnp.asarray(drawn.astype(out[name].dtype))
    for name, factor in factors.items():
        out[name] = (out[name] * factor).astype(out[name].dtype)
    return out
```

```python
from contextlib import ExitStack

import concourse.bass as bass
from concourse import mybir

F32 = mybir.dt.float32
BF16 = mybir.dt.bfloat16
I32 = mybir.dt.int32
ALU = mybir.AluOpType
ACT = mybir.ActivationFunctionType

P = 128
MASKED = -1e30
LOWEST = -3e38
EPS = 1e-5
TOPK = 16
ALPHA = {"L0": 0.1, "L1.0": 0.2, "L1.1": 0.2, "L1.2": 0.2, "L2": 0.2}
SLOTS = 2


class Events:

    def __init__(self, sems, events, first=0):
        self.sems, self.first, self.base, total = sems, first, {}, 0
        for key, count in events:
            self.base[key] = total
            total += count
        self.per_batch = total

    def index(self, key, n=0):
        return self.base[key] + n

    def value(self, it, key, n=0):
        return it * self.per_batch + (self.first + self.base[key] + n + 1)


def build(nc, x, adj, w0, a01, a02, attn_w, attn_b, w1, b1, w2, b2, g1, beta1, g2, beta2,
          w2g, a2g, wq, wk, wv, wo, out):
    B, N, D = x.shape
    L, _, F = w1.shape
    NT = N // P
    DC = D // P
    FC = F // P
    NH = 8
    DK = D // NH
    HPC = P // DK
    DA = D + 2
    PAIRS = B // SLOTS
    L1K = [f"L1.{l}" for l in range(L)]
    ATT = ["L0"] + L1K + ["L2"]
    HEADS = [f"head{h}" for h in range(NH)]

    order = []

    def add(slot, key, *stages):
        order.extend((slot, stage, key) for stage in stages)

    A, Bs = 0, 1
    add(A, "L0", "masks", "xT", "hid", "bc")
    add(Bs, "L0", "masks", "xT", "hid", "bc")
    add(A, "L0", "pT", "agg")
    add(Bs, "L0", "pT", "agg")
    add(A, "L1.0", "xT", "s", "bc")
    add(A, "L1.0", "pT", "agg")

    def weave(f, fk, a, ak):
        mid = "s" if ak in L1K else "hid"
        add(f, fk, "hT", "ffn1a")
        add(a, ak, "xT")
        add(f, fk, "ffn1b")
        add(a, ak, mid, "bc")
        add(f, fk, "ffn2a")
        add(a, ak, "pT", "agg")
        add(f, fk, "ffn2b")

    for l in range(L):
        weave(A, L1K[l], Bs, L1K[l])
        weave(Bs, L1K[l], A, (L1K + ["L2"])[l + 1])
    add(A, "L3", "xT", "qkv")
    add(Bs, "L2", "xT", "hid", "bc")
    add(A, HEADS[0], "scores")
    add(Bs, "L2", "pT", "agg")
    add(A, HEADS[0], "pT", "pv")
    add(Bs, "L3", "xT", "qkv")
    for h in range(1, NH):
        add(A, HEADS[h], "scores")
        if h > 1:
            add(Bs, HEADS[h - 2], "pT", "pv")
        add(Bs, HEADS[h - 1], "scores")
        add(A, HEADS[h], "pT", "pv")
    add(Bs, HEADS[NH - 2], "pT", "pv")
    add(Bs, HEADS[NH - 1], "scores")
    add(A, "L3", "norm", "proj")
    add(Bs, HEADS[NH - 1], "pT", "pv")
    add(Bs, "L3", "norm", "proj")

    with ExitStack() as ctx:
        def sb(name, shape, dt=F32):
            return ctx.enter_context(nc.sbuf_tensor(name, shape, dt))

        def pair(name, shape, dt=F32):
            return [sb(f"{name}_{s}", shape, dt) for s in range(SLOTS)]

        def sem(name):
            return ctx.enter_context(nc.semaphore(name))

        def signal(name, events, first=0):
            return Events([sem(f"{name}_{s}") for s in range(SLOTS)], events, first)

        ident = sb("ident", [P, P])
        no_diag = sb("no_diag", [P, P], BF16)
        minus_half = sb("minus_half", [P, NT])
        w0_sb = sb("w0_sb", [P, DC, DA])
        wg_sb = sb("wg_sb", [P, DC, DA])
        aw_sb = sb("aw_sb", [P, L, DC, 2])
        ab_sb = sb("ab_sb", [P, L, NT, 2])
        w1_sb = sb("w1_sb", [P, L, DC, F])
        b1_sb = sb("b1_sb", [P, L, FC])
        w2_sb = sb("w2_sb", [P, L, FC, D])
        g1t_sb = sb("g1t_sb", [P, L, DC])
        beta1t_sb = sb("beta1t_sb", [P, L, DC])
        g1_sb = sb("g1_sb", [P, L, D])
        c1_sb = sb("c1_sb", [P, L, D])
        g2_sb = sb("g2_sb", [P, L, D])
        beta2_sb = sb("beta2_sb", [P, L, D])
        wq_sb = sb("wq_sb", [P, DC, D])
        wk_sb = sb("wk_sb", [P, DC, D])
        wv_sb = sb("wv_sb", [P, DC, D])
        wo_sb = sb("wo_sb", [P, DC, D])
        gT = sb("gT", [P, FC, N])

        HX = pair("HX", [P, NT, D])
        X = pair("X", [P, NT, D])
        X1 = pair("X1", [P, NT, D])
        R = pair("R", [P, NT, D])
        XT = pair("XT", [P, DC, N])
        V = pair("V", [P, NT, DA])
        T = pair("T", [P, NT, N])
        PT = pair("PT", [P, NT, N])
        neg0 = pair("neg0", [P, NT, N], BF16)
        neg1 = pair("neg1", [P, NT, N], BF16)
        s12 = pair("s12", [P, NT, 2])
        row_max = pair("row_max", [P, NT])
        neg_z = pair("neg_z", [P, NT])
        alpha_target = pair("alpha_target", [P, NT])
        neg_max = pair("neg_max", [P, NT])
        den = pair("den", [P, NT])
        rden = pair("rden", [P, NT])
        top = pair("top", [P, NT, TOPK])
        stats = pair("stats", [P, NT, 6])
        mean_var = pair("mean_var", [P, NT, 2])
        var_eps = pair("var_eps", [P, NT])
        rstd = pair("rstd", [P, NT])
        has_edge = pair("has_edge", [P, NT])
        edge_nan = pair("edge_nan", [P, NT])
        den3 = pair("den3", [P, NT, NH])
        rden3 = pair("rden3", [P, NT, NH])

        QT = [R[s][:].rearrange("p a b -> p (a b)").rearrange("p (c n) -> p c n", c=DC) for s in range(SLOTS)]
        KT = [X[s][:].rearrange("p a b -> p (a b)").rearrange("p (c n) -> p c n", c=DC) for s in range(SLOTS)]

        work = [[ctx.enter_context(nc.psum_tensor(f"work_{s}_{i}", [P, N], F32)) for i in range(2)]
                for s in range(SLOTS)]
        acc = [[ctx.enter_context(nc.psum_tensor(f"acc_{s}_{i}", [P, 2, D], F32)) for i in range(NT // 2)]
               for s in range(SLOTS)]

        loaded = sem("loaded")
        consts = sem("consts")
        folded = sem("folded")
        held = sem("held")
        x_in = signal("x_in", [("L0", 16)])
        adj_in = signal("adj_in", [("L0", 16)])
        sent = signal("sent", [("L3", 16)], first=16)
        masked = signal("masked", [("L0", 3)])

        uses = []
        for k in ATT:
            uses += [(f"xT {k}", DC), (f"s {k}", 1) if k in L1K else (f"v {k}", NT), (f"bc {k}", 1), (f"pT {k}", NT)]
            if k in L1K:
                uses += [(f"hT {k}", DC), (f"g {k}", FC)]
        uses += [("xT L3", DC), ("q L3", DC), ("k L3", DC), ("v L3", NT)]
        for k in HEADS:
            uses += [(f"scores {k}", NT), (f"pT {k}", NT)]
        uses += [("oT L3", DC)]
        turn = Events(None, uses)
        assert turn.per_batch % 2 == 0
        per_bank = turn.per_batch // 2
        filled = [[sem(f"filled_{s}_{i}") for i in range(2)] for s in range(SLOTS)]
        evacuated = [[sem(f"evacuated_{s}_{i}") for i in range(2)] for s in range(SLOTS)]

        acc_uses = [("L0", 1)] + [(k + c, 1) for k in L1K for c in ("", " ffn")] + [("L2", 1), ("heads", 1), ("L3", 1)]
        acc_filled = signal("acc_filled", acc_uses)
        acc_evacuated = signal("acc_evacuated", acc_uses, first=1)

        neg_z_ready = signal("neg_z_ready", [(k, 1) for k in ATT])
        neg_max_ready = signal("neg_max_ready", [(k, 1) for k in ATT + HEADS])
        edge_step = signal("edge_step", [("L0", 3)])
        topk_step = signal("topk_step", [("L2", 3 * NT)])
        alpha_target_ready = signal("alpha_target_ready", [(k, 1) for k in ATT])
        alpha_z_done = signal("alpha_z_done", [(k, NT) for k in ATT])
        lrelu_done = signal("lrelu_done", [(k, NT) for k in ATT])
        exp_done = signal("exp_done", [(k, NT) for k in ATT + HEADS])
        kept = signal("kept", [("L2", NT)])
        rden_ready = signal("rden_ready", [(k, 1) for k in ATT + ["L3"]])
        elu_step = signal("elu_step", [("L0", 2), ("L2", 2)])
        sum_ready = signal("sum_ready", [(k, 1) for k in ("L0", "L1", "L2")])
        norms = [(k, 1) for k in ["L0"] + [q + c for q in L1K for c in (" h", " x")] + ["L1", "L2", "L3"]]
        stats_ready = signal("stats_ready", norms)
        mean_ready = signal("mean_ready", norms)
        var_ready = signal("var_ready", norms)
        rstd_ready = signal("rstd_ready", norms)
        normed = signal("normed", norms)
        affine_half = signal("affine_half", [(k + c, 1) for k in L1K for c in (" h", " x")])
        affine_done = signal("affine_done", [(k + c, 1) for k in L1K for c in (" h", " x")])

        def hold(dve):
            dve.sem_inc(held, 1)

        class Use:

            def __init__(self, s, it, key, n=0):
                i = turn.index(key, n)
                self.bank = work[s][i % 2]
                self.filled, self.evacuated = filled[s][i % 2], evacuated[s][i % 2]
                self.turn = it * per_bank + (i // 2 + 1)

        def target_score(s, key, t):
            return s12[s][:, t, 0:1] if key in L1K else V[s][:, t, D:D + 1]

        SOURCE = {"L0": HX, "L1.0": X1, "L1.1": X, "L1.2": X, "L2": X1, "L3": X1}

        def wait_source(eng, s, it, key):
            if key == "L0":
                eng.wait_ge(x_in.sems[s], x_in.value(it, "L0", 15))
            elif key in ("L1.1", "L1.2"):
                eng.wait_ge(affine_done.sems[s], affine_done.value(it, L1K[L1K.index(key) - 1] + " x"))
            else:
                eng.wait_ge(normed.sems[s], normed.value(it, {"L1.0": "L0", "L2": "L1", "L3": "L2"}[key]))

        def walk(it, stages):
            for s, stage, key in order:
                if stage in stages:
                    stages[stage](s, it, key)

        N_LOADS = 6 + L * (2 * DC + 5 + 5) + 4
        N_CONSTS = 5
        N_FOLDED = 4 * DC + 2 * L + 1

        block = ctx.enter_context(nc.Block())

        @block.sync
        def _(sp):
            n_loads = [0]

            def load(dst, src):
                sp.dma_start(dst, src).then_inc(loaded, 16)
                n_loads[0] += 1

            def load_columns(dst, src):
                sp.dma_start(dst, src.rearrange("(c p) -> p c", p=P), allow_slow_non_contiguous=True)\
                    .then_inc(loaded, 16)
                n_loads[0] += 1

            def load_x(s, it):
                sp.dma_start(HX[s][:], x[it * SLOTS + s].rearrange("(t p) d -> p t d", p=P)).then_inc(x_in.sems[s], 16)

            def row(src):
                return src.rearrange("(o d) one -> o (d one)", o=1)

            for s in range(SLOTS):
                sp.sem_inc(sent.sems[s], 16)
            load_x(0, 0)
            load(w0_sb[:, :, 0:D], w0.rearrange("(c p) n -> p c n", p=P))
            load(gT[:, 0, 0:D], row(a01).broadcast_to([P, D]))
            load(gT[:, 1, 0:D], row(a02).broadcast_to([P, D]))
            load(gT[:, 2, 0:2 * D], row(a2g).broadcast_to([P, 2 * D]))
            load(gT[:, 3, 0:L], attn_b.rearrange("(o l) -> o l", o=1).broadcast_to([P, L]))
            load(wg_sb[:, :, 0:D], w2g.rearrange("(c p) n -> p c n", p=P))
            load_x(1, 0)
            for l in range(L):
                for half in range(2):
                    for c in range(DC):
                        load(aw_sb[:, l, c, half:half + 1],
                             attn_w[l, half * D + c * P:half * D + (c + 1) * P].rearrange("(p one) -> p one", one=1))
                load(w1_sb[:, l], w1[l].rearrange("(c p) f -> p c f", p=P))
                load(w2_sb[:, l], w2[l].rearrange("(c p) n -> p c n", p=P))
                load_columns(b1_sb[:, l], b1[l])
                load_columns(g1t_sb[:, l], g1[l])
                load_columns(beta1t_sb[:, l], beta1[l])
                for dst, src in ((g1_sb[:, l], g1), (c1_sb[:, l], beta1), (gT[:, 4 + l, 0:D], b2),
                                 (g2_sb[:, l], g2), (beta2_sb[:, l], beta2)):
                    load(dst, src[l:l + 1, :].broadcast_to([P, D]))
            for dst, src in ((wq_sb, wq), (wk_sb, wk), (wv_sb, wv), (wo_sb, wo)):
                load(dst[:], src.rearrange("(c p) n -> p c n", p=P))
            assert n_loads[0] == N_LOADS

            def store(s, it):
                sp.wait_ge(normed.sems[s], normed.value(it, "L3"))
                sp.dma_start(out[it * SLOTS + s].rearrange("(t p) d -> p t d", p=P), X[s][:]).then_inc(sent.sems[s], 16)

            with sp.Fori(0, PAIRS - 1) as it:
                for s in range(SLOTS):
                    sp.wait_ge(normed.sems[s], normed.value(it, "L1"))
                    load_x(s, it + 1)
                for s in range(SLOTS):
                    store(s, it)
            for s in range(SLOTS):
                store(s, PAIRS - 1)
            for s in range(SLOTS):
                sp.wait_ge(sent.sems[s], sent.value(PAIRS - 1, "L3", 15))

        @block.gpsimd
        def _(pool):
            def load_adj(s, it):
                pool.dma_start(neg1[s][:], adj[it * SLOTS + s].rearrange("(t p) j -> p t j", p=P))\
                    .then_inc(adj_in.sems[s], 16)

            for s in range(SLOTS):
                load_adj(s, 0)
            pool.memset(ident[:], 0.0).then_inc(consts, 1)
            pool.memset(no_diag[:], 1.0).then_inc(consts, 1)
            pool.memset(minus_half[:], -0.5).then_inc(consts, 1)
            pool.wait_ge(consts, 3)
            for m, fill_with in ((ident, 1.0), (no_diag, 0.0)):
                pool.affine_select(out=m[:], in_=m[:], compare_op=ALU.not_equal, fill=fill_with, base=0,
                                   pattern=[[-1, P]], channel_multiplier=1).then_inc(consts, 1)
            pool.wait_ge(consts, N_CONSTS)
            pool.wait_ge(folded, N_FOLDED)

            def rsqrt(s, it, key):
                pool.wait_ge(var_ready.sems[s], var_ready.value(it, key))
                pool.tensor_tensor(rstd[s][:], var_eps[s][:], minus_half[:], ALU.pow).then_inc(rstd_ready.sems[s], 1)

            def affine(s, it, key, dst, src, gain, shift):
                l = L1K.index(key[:4])
                pool.wait_ge(normed.sems[s], normed.value(it, key))
                pool.tensor_tensor(dst[:], src[:], gain[:, l:l + 1, :].broadcast_to([P, NT, D]), ALU.mult)\
                    .then_inc(affine_half.sems[s], 1)
                pool.wait_ge(affine_half.sems[s], affine_half.value(it, key))
                pool.tensor_tensor(dst[:], dst[:], shift[:, l:l + 1, :].broadcast_to([P, NT, D]), ALU.add)\
                    .then_inc(affine_done.sems[s], 1)

            def agg(s, it, key):
                if key in L1K:
                    rsqrt(s, it, key + " h")
                    affine(s, it, key + " h", R[s], HX[s], g1_sb, c1_sb)
                else:
                    rsqrt(s, it, key)

            def ffn2b(prefetch):
                def stage(s, it, key):
                    rsqrt(s, it, key + " x")
                    affine(s, it, key + " x", X[s], X[s], g2_sb, beta2_sb)
                    if key == L1K[-1]:
                        rsqrt(s, it, "L1")
                        if prefetch:
                            load_adj(s, it + 1)
                return stage

            with pool.Fori(0, PAIRS - 1) as it:
                walk(it, {"agg": agg, "ffn2b": ffn2b(True), "proj": rsqrt})
            walk(PAIRS - 1, {"agg": agg, "ffn2b": ffn2b(False), "proj": rsqrt})

        @block.vector
        def _(dve):
            dve.wait_ge(loaded, 16 * N_LOADS)
            for c in range(DC):
                for half in range(2):
                    dve.tensor_tensor_reduce(X1[half][:, c, :], w0_sb[:, c, 0:D], gT[:, half, 0:D], 1.0, 0.0,
                                             ALU.mult, ALU.add, w0_sb[:, c, D + half:D + half + 1]).then_inc(folded, 1)
                    dve.tensor_tensor_reduce(X1[half][:, DC + c, :], wg_sb[:, c, 0:D], gT[:, 2, half * D:(half + 1) * D],
                                             1.0, 0.0, ALU.mult, ALU.add,
                                             wg_sb[:, c, D + half:D + half + 1]).then_inc(folded, 1)
            for l in range(L):
                dve.tensor_tensor(c1_sb[:, l], c1_sb[:, l], gT[:, 4 + l, 0:D], ALU.add).then_inc(folded, 1)
            dve.memset(ab_sb[:], 0.0).then_inc(folded, 1)
            dve.wait_ge(folded, 4 * DC + L + 1)
            for l in range(L):
                dve.tensor_copy(ab_sb[:, l, :, 0], gT[:, 3, l:l + 1].broadcast_to([P, NT])).then_inc(folded, 1)
            dve.wait_ge(folded, N_FOLDED)
            dve.wait_ge(consts, N_CONSTS)
            for s in range(SLOTS):
                dve.memset(den[s][:], 0.0).then_inc(evacuated[s][0], 1)
                dve.memset(rden[s][:], 0.0).then_inc(evacuated[s][1], 1)
                dve.memset(neg_z[s][:], 0.0).then_inc(acc_evacuated.sems[s], 1)

            def make_masks(s, it, key):
                dve.wait_ge(adj_in.sems[s], adj_in.value(it, "L0", 15))
                dve.tensor_scalar(neg0[s][:], neg1[s][:], 0.0, MASKED, ALU.is_equal, ALU.mult).then_inc(masked.sems[s], 1)
                dve.wait_ge(masked.sems[s], masked.value(it, "L0", 0))
                dve.tensor_copy(neg1[s][:], neg0[s][:]).then_inc(masked.sems[s], 1)
                dve.wait_ge(masked.sems[s], masked.value(it, "L0", 1))
                for t in range(NT):
                    last = dve.tensor_tensor(neg1[s][:, t, t * P:(t + 1) * P], neg0[s][:, t, t * P:(t + 1) * P],
                                             no_diag[:], ALU.mult)
                last.then_inc(masked.sems[s], 1)
                dve.wait_ge(masked.sems[s], masked.value(it, "L0", 2))

            def x_transposed(s, it, key):
                u = Use(s, it, f"xT {key}", 1)
                dve.wait_ge(u.filled, u.turn)
                dve.tensor_copy(XT[s][:, 1, :], u.bank[:]).then_inc(u.evacuated, 1)

            def scores_of_x(s, it, key):
                u = Use(s, it, f"s {key}")
                dve.wait_ge(u.filled, u.turn)
                dve.tensor_tensor(s12[s][:], u.bank[:, 0:NT * 2].rearrange("p (t k) -> p t k", k=2),
                                  ab_sb[:, L1K.index(key)], ALU.add).then_inc(u.evacuated, 1)

            def masked_max(s, it, key):
                u = Use(s, it, f"bc {key}")
                dve.wait_ge(u.filled, u.turn)
                neg = neg1 if key in L1K else neg0
                hold(dve)
                for t in range(NT):
                    last = dve.tensor_tensor_reduce(T[s][:, t, :], u.bank[:], neg[s][:, t, :], 1.0, LOWEST,
                                                    ALU.add, ALU.max, row_max[s][:, t:t + 1])
                last.then_inc(u.evacuated, 1)
                u = Use(s, it, f"bc {key}")
                dve.wait_ge(u.evacuated, u.turn + 1)
                target = s12[s][:, :, 0] if key in L1K else V[s][:, :, D]
                dve.scalar_tensor_tensor(neg_z[s][:], row_max[s][:], -1.0, target, ALU.mult, ALU.subtract)\
                    .then_inc(neg_z_ready.sems[s], 1)
                if key == "L0":
                    dve.tensor_scalar(has_edge[s][:], row_max[s][:], 0.5 * MASKED, None, ALU.is_gt)\
                        .then_inc(edge_step.sems[s], 1)
                    dve.wait_ge(edge_step.sems[s], edge_step.value(it, "L0", 0))
                    dve.reciprocal(edge_nan[s][:], has_edge[s][:]).then_inc(edge_step.sems[s], 1)
                    dve.wait_ge(edge_step.sems[s], edge_step.value(it, "L0", 1))
                    dve.tensor_tensor(edge_nan[s][:], edge_nan[s][:], has_edge[s][:], ALU.mult)\
                        .then_inc(edge_step.sems[s], 1)
                if key == "L2":
                    for t in range(NT):
                        dve.max(top[s][:, t, 0:8], T[s][:, t, :]).then_inc(topk_step.sems[s], 1)
                    for t in range(NT):
                        dve.wait_ge(topk_step.sems[s], topk_step.value(it, "L2", t))
                        hold(dve)
                        dve.match_replace(PT[s][:, t, :], top[s][:, t, 0:8], T[s][:, t, :], LOWEST)\
                            .then_inc(topk_step.sems[s], 1)
                    for t in range(NT):
                        dve.wait_ge(topk_step.sems[s], topk_step.value(it, "L2", NT + t))
                        hold(dve)
                        dve.max(top[s][:, t, 8:16], PT[s][:, t, :]).then_inc(topk_step.sems[s], 1)
                    dve.wait_ge(topk_step.sems[s], topk_step.value(it, "L2", 3 * NT - 1))
                dve.tensor_scalar(alpha_target[s][:], target, ALPHA[key], None, ALU.mult)\
                    .then_inc(alpha_target_ready.sems[s], 1)
                dve.wait_ge(neg_z_ready.sems[s], neg_z_ready.value(it, key))
                dve.scalar_tensor_tensor(neg_max[s][:], neg_z[s][:], ALPHA[key], neg_z[s][:], ALU.mult, ALU.min)\
                    .then_inc(neg_max_ready.sems[s], 1)
                for t in range(NT):
                    dve.wait_ge(alpha_z_done.sems[s], alpha_z_done.value(it, key, t))
                    dve.scalar_tensor_tensor(PT[s][:, t, :], T[s][:, t, :], target_score(s, key, t), PT[s][:, t, :],
                                             ALU.add, ALU.max).then_inc(lrelu_done.sems[s], 1)

            def weights_transposed(s, it, key):
                if key == "L2":
                    for t in range(NT):
                        dve.wait_ge(exp_done.sems[s], exp_done.value(it, key, t))
                        dve.scalar_tensor_tensor(T[s][:, t, :], T[s][:, t, :], top[s][:, t, TOPK - 1:TOPK],
                                                 PT[s][:, t, :], ALU.is_ge, ALU.mult).then_inc(kept.sems[s], 1)
                if key in ATT:
                    dve.wait_ge(exp_done.sems[s], exp_done.value(it, key, NT - 1))
                    dve.reciprocal(rden[s][:], den[s][:]).then_inc(rden_ready.sems[s], 1)
                for j in range(1, NT, 2):
                    u = Use(s, it, f"pT {key}", j)
                    dve.wait_ge(u.filled, u.turn)
                    dve.tensor_copy(PT[s][:, j, :], u.bank[:]).then_inc(u.evacuated, 1)

            def layer_norm(s, it, key, dst):
                for t in range(NT):
                    last = dve.bn_stats(stats[s][:, t, :], R[s][:, t, :])
                last.then_inc(stats_ready.sems[s], 1)
                dve.wait_ge(stats_ready.sems[s], stats_ready.value(it, key))
                hold(dve)
                for t in range(NT):
                    last = dve.bn_aggr(mean_var[s][:, t, :], stats[s][:, t, :])
                last.then_inc(mean_ready.sems[s], 1)
                dve.wait_ge(mean_ready.sems[s], mean_ready.value(it, key))
                dve.tensor_scalar(var_eps[s][:], mean_var[s][:, :, 1], EPS, None, ALU.add).then_inc(var_ready.sems[s], 1)
                dve.wait_ge(rstd_ready.sems[s], rstd_ready.value(it, key))
                for t in range(NT):
                    last = dve.tensor_scalar(dst[:, t, :], R[s][:, t, :], mean_var[s][:, t, 0:1], rstd[s][:, t:t + 1],
                                             ALU.subtract, ALU.mult)
                last.then_inc(normed.sems[s], 1)

            def agg(s, it, key):
                if key in L1K:
                    wait_source(dve, s, it, key)
                    dve.wait_ge(rden_ready.sems[s], rden_ready.value(it, key))
                    dve.wait_ge(acc_filled.sems[s], acc_filled.value(it, key))
                    for t in range(NT):
                        last = dve.scalar_tensor_tensor(R[s][:, t, :], acc[s][t // 2][:, t % 2, :], rden[s][:, t:t + 1],
                                                        SOURCE[key][s][:, t, :], ALU.mult, ALU.add)
                    last.then_inc(acc_evacuated.sems[s], 1)
                    dve.wait_ge(acc_evacuated.sems[s], acc_evacuated.value(it, key))
                    layer_norm(s, it, key + " h", HX[s])
                else:
                    E = T[s][:, :, 0:D]
                    dve.wait_ge(acc_evacuated.sems[s], acc_evacuated.value(it, key))
                    dve.tensor_scalar(E, E, 1.0, -1.0, ALU.min, ALU.add).then_inc(elu_step.sems[s], 1)
                    dve.wait_ge(elu_step.sems[s], elu_step.value(it, key, 0))
                    dve.tensor_tensor(R[s][:], R[s][:], E, ALU.max).then_inc(elu_step.sems[s], 1)
                    dve.wait_ge(elu_step.sems[s], elu_step.value(it, key, 1))
                    dve.tensor_tensor(R[s][:], R[s][:], SOURCE[key][s][:], ALU.add).then_inc(sum_ready.sems[s], 1)
                    dve.wait_ge(sum_ready.sems[s], sum_ready.value(it, key))
                    layer_norm(s, it, key, X1[s])

            def h_transposed(s, it, key):
                l = L1K.index(key)
                u = Use(s, it, f"hT {key}", 1)
                dve.wait_ge(u.filled, u.turn)
                dve.tensor_scalar(XT[s][:, 1, :], u.bank[:], g1t_sb[:, l, 1:2], beta1t_sb[:, l, 1:2], ALU.mult, ALU.add)\
                    .then_inc(u.evacuated, 1)

            def after_ffn(s, it, key):
                dve.wait_ge(affine_done.sems[s], affine_done.value(it, key + " h"))
                dve.wait_ge(acc_filled.sems[s], acc_filled.value(it, key + " ffn"))
                for i in range(NT // 2):
                    last = dve.tensor_tensor(R[s][:, 2 * i:2 * i + 2, :], acc[s][i][:], R[s][:, 2 * i:2 * i + 2, :],
                                             ALU.add)
                last.then_inc(acc_evacuated.sems[s], 1)
                dve.wait_ge(acc_evacuated.sems[s], acc_evacuated.value(it, key + " ffn"))
                if key == L1K[0]:
                    dve.wait_ge(sent.sems[s], it * 16 + 16)
                layer_norm(s, it, key + " x", X[s])
                if key == L1K[-1]:
                    dve.wait_ge(affine_done.sems[s], affine_done.value(it, key + " x"))
                    dve.tensor_tensor(R[s][:], X[s][:], X1[s][:], ALU.add).then_inc(sum_ready.sems[s], 1)
                    dve.wait_ge(sum_ready.sems[s], sum_ready.value(it, "L1"))
                    layer_norm(s, it, "L1", X1[s])

            def qkv(s, it, key):
                for c in range(DC):
                    u = Use(s, it, "k L3", c)
                    dve.wait_ge(u.filled, u.turn)
                    dve.tensor_copy(KT[s][:, c, :], u.bank[:]).then_inc(u.evacuated, 1)

            def head_scores(s, it, key):
                for t in range(NT):
                    u = Use(s, it, f"scores {key}", t)
                    dve.wait_ge(u.filled, u.turn)
                    hold(dve)
                    dve.tensor_tensor_reduce(T[s][:, t, :], u.bank[:], neg0[s][:, t, :], 1.0, LOWEST, ALU.add, ALU.max,
                                             row_max[s][:, t:t + 1]).then_inc(u.evacuated, 1)
                u = Use(s, it, f"scores {key}", NT - 2)
                dve.wait_ge(u.evacuated, u.turn + 1)
                u = Use(s, it, f"scores {key}", NT - 1)
                dve.wait_ge(u.evacuated, u.turn + 1)
                dve.tensor_scalar(neg_max[s][:], row_max[s][:], -1.0, None, ALU.mult).then_inc(neg_max_ready.sems[s], 1)

            def head_outputs(s, it, key):
                dve.wait_ge(exp_done.sems[s], exp_done.value(it, HEADS[-1], NT - 1))
                dve.reciprocal(rden3[s][:], den3[s][:]).then_inc(rden_ready.sems[s], 1)
                dve.wait_ge(rden_ready.sems[s], rden_ready.value(it, "L3"))
                dve.wait_ge(acc_filled.sems[s], acc_filled.value(it, "heads"))
                for i in range(NT // 2):
                    per_head = rden3[s][:, 2 * i:2 * i + 2, :].rearrange("p t (h o) -> p (t h) o", o=1)
                    last = dve.tensor_tensor(
                        R[s][:, 2 * i:2 * i + 2, :].rearrange("p t (h k) -> p (t h) k", k=DK),
                        acc[s][i][:].rearrange("p t (h k) -> p (t h) k", k=DK),
                        per_head.broadcast_to([P, 2 * NH, DK]), ALU.mult)
                last.then_inc(acc_evacuated.sems[s], 1)
                u = Use(s, it, "oT L3", 1)
                dve.wait_ge(u.filled, u.turn)
                dve.tensor_scalar(XT[s][:, 1, :], u.bank[:], 0.0, None, ALU.max).then_inc(u.evacuated, 1)

            def after_proj(s, it, key):
                dve.wait_ge(acc_filled.sems[s], acc_filled.value(it, "L3"))
                for t in range(NT):
                    last = dve.scalar_tensor_tensor(R[s][:, t, :], X1[s][:, t, :], edge_nan[s][:, t:t + 1],
                                                    acc[s][t // 2][:, t % 2, :], ALU.mult, ALU.add)
                last.then_inc(acc_evacuated.sems[s], 1)
                dve.wait_ge(acc_evacuated.sems[s], acc_evacuated.value(it, "L3"))
                layer_norm(s, it, "L3", X[s])

            with dve.Fori(0, PAIRS) as it:
                walk(it, {"masks": make_masks, "xT": x_transposed, "s": scores_of_x, "bc": masked_max,
                          "pT": weights_transposed, "agg": agg, "hT": h_transposed, "ffn2b": after_ffn, "qkv": qkv,
                          "scores": head_scores, "norm": head_outputs, "proj": after_proj})

        @block.scalar
        def _(act):
            act.wait_ge(loaded, 16 * N_LOADS)
            act.wait_ge(folded, N_FOLDED)

            def x_transposed(s, it, key):
                u = Use(s, it, f"xT {key}", 0)
                act.wait_ge(u.filled, u.turn)
                act.activation(XT[s][:, 0, :], u.bank[:], ACT.Copy).then_inc(u.evacuated, 1)

            def projected(s, it, key):
                for t in range(NT):
                    u = Use(s, it, f"v {key}", t)
                    act.wait_ge(u.filled, u.turn)
                    act.activation(V[s][:, t, :], u.bank[:, 0:DA], ACT.Copy).then_inc(u.evacuated, 1)

            def softmax(s, it, key):
                act.wait_ge(alpha_target_ready.sems[s], alpha_target_ready.value(it, key))
                for t in range(NT):
                    act.activation(PT[s][:, t, :], T[s][:, t, :], ACT.Identity, bias=alpha_target[s][:, t:t + 1],
                                   scale=ALPHA[key]).then_inc(alpha_z_done.sems[s], 1)
                dst = PT if key == "L2" else T
                for t in range(NT):
                    act.wait_ge(lrelu_done.sems[s], lrelu_done.value(it, key, t))
                    act.activation(dst[s][:, t, :], PT[s][:, t, :], ACT.Exp, bias=neg_max[s][:, t:t + 1],
                                   accum_out=den[s][:, t:t + 1]).then_inc(exp_done.sems[s], 1)

            def weights_transposed(s, it, key):
                for j in range(0, NT, 2):
                    u = Use(s, it, f"pT {key}", j)
                    act.wait_ge(u.filled, u.turn)
                    act.activation(PT[s][:, j, :], u.bank[:], ACT.Copy).then_inc(u.evacuated, 1)

            def agg(s, it, key):
                if key in L1K:
                    return
                act.wait_ge(rden_ready.sems[s], rden_ready.value(it, key))
                act.wait_ge(acc_filled.sems[s], acc_filled.value(it, key))
                for t in range(NT):
                    act.activation(R[s][:, t, :], acc[s][t // 2][:, t % 2, :], ACT.Copy, scale=rden[s][:, t:t + 1])
                for t in range(NT):
                    last = act.activation(T[s][:, t, 0:D], acc[s][t // 2][:, t % 2, :], ACT.Exp,
                                          scale=rden[s][:, t:t + 1])
                last.then_inc(acc_evacuated.sems[s], 1)

            def h_transposed(s, it, key):
                l = L1K.index(key)
                u = Use(s, it, f"hT {key}", 0)
                act.wait_ge(u.filled, u.turn)
                act.activation(XT[s][:, 0, :], u.bank[:], ACT.Identity, scale=g1t_sb[:, l, 0:1],
                               bias=beta1t_sb[:, l, 0:1]).then_inc(u.evacuated, 1)

            def gelu(part):
                def stage(s, it, key):
                    l = L1K.index(key)
                    for f in part:
                        u = Use(s, it, f"g {key}", f)
                        act.wait_ge(u.filled, u.turn)
                        act.activation(gT[:, f, :], u.bank[:], ACT.Gelu, bias=b1_sb[:, l, f:f + 1]).then_inc(u.evacuated, 1)
                return stage

            def qkv(s, it, key):
                for c in range(DC):
                    u = Use(s, it, "q L3", c)
                    act.wait_ge(u.filled, u.turn)
                    act.activation(QT[s][:, c, :], u.bank[:], ACT.Copy, scale=float(DK) ** -0.5).then_inc(u.evacuated, 1)
                for t in range(NT):
                    u = Use(s, it, "v L3", t)
                    act.wait_ge(u.filled, u.turn)
                    act.activation(V[s][:, t, 0:D], u.bank[:, 0:D], ACT.Copy).then_inc(u.evacuated, 1)

            def head_exp(s, it, key):
                act.wait_ge(neg_max_ready.sems[s], neg_max_ready.value(it, key))
                h = HEADS.index(key)
                for t in range(NT):
                    act.activation(T[s][:, t, :], T[s][:, t, :], ACT.Exp, bias=neg_max[s][:, t:t + 1],
                                   accum_out=den3[s][:, t, h:h + 1]).then_inc(exp_done.sems[s], 1)

            def outputs_transposed(s, it, key):
                u = Use(s, it, "oT L3", 0)
                act.wait_ge(u.filled, u.turn)
                act.activation(XT[s][:, 0, :], u.bank[:], ACT.Relu).then_inc(u.evacuated, 1)

            with act.Fori(0, PAIRS) as it:
                walk(it, {"xT": x_transposed, "hid": projected, "bc": softmax, "pT": weights_transposed, "agg": agg,
                          "hT": h_transposed, "ffn1a": gelu(range(FC // 2)), "ffn1b": gelu(range(FC // 2, FC)),
                          "qkv": qkv, "scores": head_exp, "norm": outputs_transposed})

        @block.tensor
        def _(pe):
            pe.wait_ge(loaded, 16 * N_LOADS)
            pe.wait_ge(consts, N_CONSTS)
            pe.wait_ge(folded, N_FOLDED)

            def transpose_tiles(s, it, key, n, src, c):
                u = Use(s, it, key, n)
                pe.wait_ge(u.evacuated, u.turn)
                for t in range(NT):
                    last = pe.transpose(u.bank[:, t * P:(t + 1) * P], src[:, t, c * P:(c + 1) * P], ident[:])
                last.then_inc(u.filled, 1)

            def xT(s, it, key):
                wait_source(pe, s, it, key)
                for c in range(DC):
                    transpose_tiles(s, it, f"xT {key}", c, SOURCE[key][s], c)

            def project(s, it, key, weights, columns):
                for t in range(NT):
                    u = Use(s, it, key, t)
                    pe.wait_ge(u.evacuated, u.turn)
                    for c in range(DC):
                        last = pe.matmul(u.bank[:, 0:columns], XT[s][:, c, t * P:(t + 1) * P], weights[:, c, 0:columns],
                                         start=(c == 0), stop=(c == DC - 1))
                    last.then_inc(u.filled, 1)

            def hid(s, it, key):
                for c in range(DC):
                    u = Use(s, it, f"xT {key}", c)
                    pe.wait_ge(u.evacuated, u.turn + 1)
                project(s, it, f"v {key}", w0_sb if key == "L0" else wg_sb, DA)

            def scores_of_x(s, it, key):
                for c in range(DC):
                    u = Use(s, it, f"xT {key}", c)
                    pe.wait_ge(u.evacuated, u.turn + 1)
                u = Use(s, it, f"s {key}")
                pe.wait_ge(u.evacuated, u.turn)
                for t in range(NT):
                    for c in range(DC):
                        last = pe.matmul(u.bank[:, 2 * t:2 * t + 2], XT[s][:, c, t * P:(t + 1) * P],
                                         aw_sb[:, L1K.index(key), c, :], start=(c == 0), stop=(c == DC - 1))
                last.then_inc(u.filled, 1)

            def broadcast(s, it, key):
                if key in L1K:
                    u = Use(s, it, f"s {key}")
                    pe.wait_ge(u.evacuated, u.turn + 1)
                else:
                    for t in range(NT - 2, NT):
                        u = Use(s, it, f"v {key}", t)
                        pe.wait_ge(u.evacuated, u.turn + 1)
                u = Use(s, it, f"bc {key}")
                pe.wait_ge(u.evacuated, u.turn)
                for t in range(NT):
                    col = s12[s][:, t, 1:2] if key in L1K else V[s][:, t, D + 1:D + 2]
                    last = pe.transpose(u.bank[:, t * P:(t + 1) * P], col.broadcast_to([P, P]), ident[:])
                last.then_inc(u.filled, 1)

            def weights_transposed(s, it, key):
                if key == "L2":
                    pe.wait_ge(kept.sems[s], kept.value(it, key, NT - 1))
                else:
                    pe.wait_ge(exp_done.sems[s], exp_done.value(it, key, NT - 1))
                for j in range(NT):
                    transpose_tiles(s, it, f"pT {key}", j, T[s], j)

            def agg(s, it, key):
                pe.wait_ge(acc_evacuated.sems[s], acc_evacuated.value(it, key) - 1)
                src = SOURCE[key] if key in L1K else V
                for j in range(NT):
                    u = Use(s, it, f"pT {key}", j)
                    pe.wait_ge(u.evacuated, u.turn + 1)
                    for t in range(NT):
                        last = pe.matmul(acc[s][t // 2][:, t % 2, :], PT[s][:, j, t * P:(t + 1) * P], src[s][:, j, 0:D],
                                         start=(j == 0 and t % 2 == 0), stop=(j == NT - 1), skip_group_check=True)
                last.then_inc(acc_filled.sems[s], 1)

            def h_transposed(s, it, key):
                pe.wait_ge(normed.sems[s], normed.value(it, key + " h"))
                for c in range(DC):
                    transpose_tiles(s, it, f"hT {key}", c, HX[s], c)

            def ffn1(part):
                def stage(s, it, key):
                    l = L1K.index(key)
                    for c in range(DC):
                        u = Use(s, it, f"hT {key}", c)
                        pe.wait_ge(u.evacuated, u.turn + 1)
                    for f in part:
                        u = Use(s, it, f"g {key}", f)
                        pe.wait_ge(u.evacuated, u.turn)
                        for c in range(DC):
                            last = pe.matmul(u.bank[:], w1_sb[:, l, c, f * P:(f + 1) * P], XT[s][:, c, :],
                                             start=(c == 0), stop=(c == DC - 1))
                        last.then_inc(u.filled, 1)
                return stage

            def ffn2(part):
                def stage(s, it, key):
                    l = L1K.index(key)
                    if part[0] == 0:
                        pe.wait_ge(acc_evacuated.sems[s], acc_evacuated.value(it, key + " ffn") - 1)
                    for f in part:
                        u = Use(s, it, f"g {key}", f)
                        pe.wait_ge(u.evacuated, u.turn + 1)
                        for t in range(NT):
                            last = pe.matmul(acc[s][t // 2][:, t % 2, :], gT[:, f, t * P:(t + 1) * P], w2_sb[:, l, f, :],
                                             start=(f == 0 and t % 2 == 0), stop=(f == FC - 1), skip_group_check=True)
                    if part[-1] == FC - 1:
                        last.then_inc(acc_filled.sems[s], 1)
                return stage

            def qkv(s, it, key):
                for c in range(DC):
                    u = Use(s, it, "xT L3", c)
                    pe.wait_ge(u.evacuated, u.turn + 1)
                for name, weights in (("q L3", wq_sb), ("k L3", wk_sb)):
                    for m in range(DC):
                        u = Use(s, it, name, m)
                        pe.wait_ge(u.evacuated, u.turn)
                        for c in range(DC):
                            last = pe.matmul(u.bank[:], weights[:, c, m * P:(m + 1) * P], XT[s][:, c, :],
                                             start=(c == 0), stop=(c == DC - 1))
                        last.then_inc(u.filled, 1)
                project(s, it, "v L3", wv_sb, D)

            def head_scores(s, it, key):
                h = HEADS.index(key)
                m, r = h // HPC, h % HPC * DK
                for t in range(NT):
                    u = Use(s, it, f"scores {key}", t)
                    pe.wait_ge(u.evacuated, u.turn)
                    pe.matmul(u.bank[:], QT[s][r:r + DK, m, t * P:(t + 1) * P], KT[s][r:r + DK, m, :],
                              start=True, stop=True).then_inc(u.filled, 1)

            def head_output(s, it, key):
                h = HEADS.index(key)
                if h == 0:
                    pe.wait_ge(acc_evacuated.sems[s], acc_evacuated.value(it, "heads") - 1)
                for j in range(NT):
                    u = Use(s, it, f"pT {key}", j)
                    pe.wait_ge(u.evacuated, u.turn + 1)
                    for t in range(NT):
                        last = pe.matmul(acc[s][t // 2][:, t % 2, h * DK:(h + 1) * DK], PT[s][:, j, t * P:(t + 1) * P],
                                         V[s][:, j, h * DK:(h + 1) * DK], start=(j == 0 and t % 2 == 0),
                                         stop=(j == NT - 1), skip_group_check=True)
                if h == NH - 1:
                    last.then_inc(acc_filled.sems[s], 1)

            def outputs_transposed(s, it, key):
                pe.wait_ge(acc_evacuated.sems[s], acc_evacuated.value(it, "heads"))
                for c in range(DC):
                    transpose_tiles(s, it, "oT L3", c, R[s], c)

            def proj(s, it, key):
                for c in range(DC):
                    u = Use(s, it, "oT L3", c)
                    pe.wait_ge(u.evacuated, u.turn + 1)
                pe.wait_ge(acc_evacuated.sems[s], acc_evacuated.value(it, "L3") - 1)
                for t in range(NT):
                    for c in range(DC):
                        last = pe.matmul(acc[s][t // 2][:, t % 2, :], XT[s][:, c, t * P:(t + 1) * P], wo_sb[:, c, :],
                                         start=(c == 0 and t % 2 == 0), stop=(c == DC - 1), skip_group_check=True)
                last.then_inc(acc_filled.sems[s], 1)

            with pe.Fori(0, PAIRS) as it:
                walk(it, {"xT": xT, "hid": hid, "s": scores_of_x, "bc": broadcast, "pT": weights_transposed, "agg": agg,
                          "hT": h_transposed, "ffn1a": ffn1(range(FC // 2)), "ffn1b": ffn1(range(FC // 2, FC)),
                          "ffn2a": ffn2(range(FC // 2)), "ffn2b": ffn2(range(FC // 2, FC)), "qkv": qkv,
                          "scores": head_scores, "pv": head_output, "norm": outputs_transposed, "proj": proj})


_INS = ["x", "adj", "L0_gnn_w", "L0_gnn_a1", "L0_gnn_a2", "L1_gnn_attn_w", "L1_gnn_attn_b", "L1_gnn_W1",
        "L1_gnn_b1", "L1_gnn_W2", "L1_gnn_b2", "L1_gnn_g1", "L1_gnn_beta1", "L1_gnn_g2", "L1_gnn_beta2",
        "L2_gnn_W", "L2_gnn_a", "L3_gnn_Wq", "L3_gnn_Wk", "L3_gnn_Wv", "L3_gnn_Wo"]


def kernel(**inputs):
    import numpy as np
    import concourse.bacc as bacc
    from concourse.bass_utils import run_bass_kernel_spmd as run

    nc = bacc.Bacc("TRN2", target_bir_lowering=False, num_devices=1)
    arrays, args = {}, []
    for name in _INS:
        a = np.ascontiguousarray(inputs[name])
        arrays[f"in_{name}"] = a
        args.append(nc.dram_tensor(f"in_{name}", a.shape, mybir.dt.from_np(a.dtype), kind="ExternalInput").ap())
    out = nc.dram_tensor("out", arrays["in_x"].shape, F32, kind="ExternalOutput").ap()
    build(nc, *args, out)
    r = run(nc, [arrays], core_ids=[0])
    return r.results[0]["out"]
```

```python
from contextlib import ExitStack

import concourse.bass as bass
from concourse import mybir

F32 = mybir.dt.float32
BF16 = mybir.dt.bfloat16
F32R = mybir.dt.float32r
I32 = mybir.dt.int32
ALU = mybir.AluOpType
ACT = mybir.ActivationFunctionType

P = 128
MASKED = -1e30
LOWEST = -3e38
EPS = 1e-5
TOPK = 16
ALPHA = {"L0": 0.1, "L1.0": 0.2, "L1.1": 0.2, "L1.2": 0.2, "L2": 0.2}
SLOTS = 2


class Batch:

    def __init__(self, it, ahead):
        self.it, self.ahead = it, ahead

    def times(self, count, plus=0):
        return self.it * count + (self.ahead * count + plus)

    def next(self):
        return Batch(self.it, self.ahead + 1)

    def is_number(self, number):
        return isinstance(self.it, int) and self.it + self.ahead == number


class Events:

    def __init__(self, sems, events, first=0):
        self.sems, self.first, self.base, total = sems, first, {}, 0
        for key, count in events:
            self.base[key] = total
            total += count
        self.per_batch = total

    def index(self, key, n=0):
        return self.base[key] + n

    def value(self, it, key, n=0):
        return it.times(self.per_batch, self.first + self.base[key] + n + 1)


def build(nc, x, adj, w0, a01, a02, attn_w, attn_b, w1, b1, w2, b2, g1, beta1, g2, beta2,
          w2g, a2g, wq, wk, wv, wo, out):
    B, N, D = x.shape
    L, _, F = w1.shape
    NT = N // P
    DC = D // P
    FC = F // P
    NH = 8
    DK = D // NH
    HPC = P // DK
    DA = D + 2
    PAIRS = B // SLOTS
    L1K = [f"L1.{l}" for l in range(L)]
    ATT = ["L0"] + L1K + ["L2"]
    HEADS = [f"head{h}" for h in range(NH)]

    A, Bs = 0, 1

    HALF = [
        ("ending", "head3", "pv"), ("ending", "head5", "scores"), ("ending", "head4", "exp"),
        ("middle", "L1.1", "ffn1b ffn2a"), ("ending", "head7", "stack"), ("middle", "L1.1", "ffn1c ffn2b"),
        ("ending", "head4", "pT"), ("ending", "head5", "exp"), ("middle", "L1.1", "ffn1d"),
        ("ending", "head6", "scores"), ("middle", "L1.1", "ffn2c ffn2d xsum"), ("ending", "head5", "pT pv"),
        ("middle", "L1.1", "xnorm"), ("ending", "head7", "scores"), ("ending", "head6", "exp pT"),
        ("middle", "L1.2", "xT s bc"), ("ending", "head7", "exp pT"), ("middle", "L1.2", "alphaz lrelu"),
        ("ending", "head7", "pv"), ("middle", "L1.2", "exp"), ("ending", "L3", "heads"),
        ("middle", "L1.2", "pT agg"), ("ending", "L3", "proj"), ("middle", "L1.2", "sum norm hT"),
        ("ending", "L3", "load ysum norm store"), ("starting", "L0", "masks xT"),
        ("middle", "L1.2", "ffn1a ffn1b ffn2a"), ("starting", "L0", "v"), ("middle", "L1.2", "ffn1c"),
        ("starting", "L0", "bc"), ("middle", "L1.2", "ffn2b"), ("starting", "L0", "alphaz"),
        ("middle", "L1.2", "ffn1d"), ("starting", "L0", "lrelu"), ("middle", "L1.2", "ffn2c"),
        ("starting", "L0", "exp"), ("middle", "L1.2", "ffn2d"), ("starting", "L0", "pT"),
        ("middle", "L1.2", "xsum xnorm"), ("starting", "L0", "agg sum norm"), ("middle", "L1", "l1sum"),
        ("starting", "L1.0", "xT s"), ("middle", "L1", "norm"), ("starting", "L1.0", "bc"), ("middle", "L2", "xT"),
        ("starting", "L1.0", "alphaz lrelu"), ("middle", "L2", "v"), ("starting", "L1.0", "exp"),
        ("middle", "L2", "bc"), ("starting", "L1.0", "pT"), ("middle", "L2", "topk"),
        ("starting", "L1.0", "agg sum norm"), ("middle", "L2", "alphaz lrelu"), ("starting", "L1.0", "hT"),
        ("middle", "L2", "exp"), ("starting", "L1.0", "ffn1a"), ("middle", "L2", "pT agg"),
        ("starting", "L1.0", "ffn1b ffn2a ffn1c"), ("middle", "L2", "sum norm"), ("starting", "L1.0", "ffn2b"),
        ("middle", "L3", "xT"), ("starting", "L1.0", "ffn1d"), ("middle", "L3", "qkv"),
        ("starting", "L1.0", "ffn2c"), ("middle", "head0", "stack"), ("starting", "L1.0", "ffn2d xsum"),
        ("middle", "head0", "scores exp"), ("starting", "L1.0", "xnorm"), ("middle", "head1", "stack"),
        ("middle", "head2", "stack"), ("middle", "head1", "scores"), ("middle", "head0", "pT"),
        ("middle", "head1", "exp"), ("starting", "L1.1", "xT"), ("middle", "head2", "scores"),
        ("starting", "L1.1", "s bc"), ("middle", "head2", "exp"), ("middle", "head1", "pT"),
        ("starting", "L1.1", "alphaz lrelu exp"), ("middle", "head1", "pv"), ("middle", "head3", "stack scores"),
        ("starting", "L1.1", "pT agg sum"), ("middle", "head2", "pT"), ("middle", "head3", "exp"),
        ("starting", "L1.1", "norm"), ("middle", "head4", "stack scores"), ("starting", "L1.1", "hT"),
        ("middle", "head3", "pT"), ("middle", "head5", "stack"), ("starting", "L1.1", "ffn1a"),
        ("middle", "head6", "stack"),
    ]

    def half_batch(middle, other, after, ending=True, starting=True):
        place = {"middle": (middle, 0), "ending": (other, after), "starting": (other, after + 1)}
        left_out = ([] if ending else ["ending"]) + ([] if starting else ["starting"])
        return [place[part] + (stage, key) for part, key, stages in HALF if part not in left_out
                for stage in stages.split()]

    def only(wanted, slot):
        return [(slot, 0, stage, key) for part, key, stages in HALF if part == wanted for stage in stages.split()]

    A, Bs = 0, 1
    opening = only("starting", A) + half_batch(A, Bs, -1, ending=False)
    to_a = half_batch(Bs, A, 0)
    to_b = half_batch(A, Bs, -1)
    closing = half_batch(Bs, A, 0, starting=False) + only("ending", Bs)

    with ExitStack() as ctx:
        def sb(name, shape, dt=F32):
            return ctx.enter_context(nc.sbuf_tensor(name, shape, dt))

        def pair(name, shape, dt=F32):
            return [sb(f"{name}_{s}", shape, dt) for s in range(SLOTS)]

        def sem(name):
            return ctx.enter_context(nc.semaphore(name))

        def signal(name, events, first=0):
            return Events([sem(f"{name}_{s}") for s in range(SLOTS)], events, first)

        ident = sb("ident", [P, P])
        no_diag = sb("no_diag", [P, P], BF16)
        minus_half = sb("minus_half", [P, NT])
        w0_sb = sb("w0_sb", [P, DC, DA])
        wg_sb = sb("wg_sb", [P, DC, DA])
        aw_sb = sb("aw_sb", [P, L, DC, 2])
        ab_sb = sb("ab_sb", [P, L, NT, 2])
        w1_sb = sb("w1_sb", [P, L, DC, F])
        b1_sb = sb("b1_sb", [P, L, FC])
        w2_sb = sb("w2_sb", [P, L, FC, D])
        g1t_sb = sb("g1t_sb", [P, L, DC])
        beta1t_sb = sb("beta1t_sb", [P, L, DC])
        g1_sb = sb("g1_sb", [P, L, D])
        c1_sb = sb("c1_sb", [P, L, D])
        g2_sb = sb("g2_sb", [P, L, D])
        beta2_sb = sb("beta2_sb", [P, L, D])
        wq_sb = sb("wq_sb", [P, DC, D])
        wk_sb = sb("wk_sb", [P, DC, D])
        wv_sb = sb("wv_sb", [P, DC, D])
        wo_sb = sb("wo_sb", [P, DC, D])
        head_rows = sb("head_rows", [NH, DC, P])

        gT = sb("gT", [P, FC // 2, N])
        PT2 = sb("PT2", [P, 2, NT, N])
        q4 = sb("q4", [P, 2, N], F32R)
        k4 = sb("k4", [P, 2, N], F32R)

        HX = pair("HX", [P, NT, D])
        X = pair("X", [P, NT, D])
        X1 = pair("X1", [P, NT, D])
        R = pair("R", [P, NT, D])
        XT = pair("XT", [P, DC, N])
        V = pair("V", [P, NT, DA])
        T = pair("T", [P, NT, N])
        PT = pair("PT", [P, NT, N])
        neg0 = pair("neg0", [P, NT, N], BF16)
        neg1 = pair("neg1", [P, NT, N], BF16)
        s12 = pair("s12", [P, NT, 2])
        row_max = pair("row_max", [P, NT])
        neg_z = pair("neg_z", [P, NT])
        alpha_target = pair("alpha_target", [P, NT])
        neg_max = pair("neg_max", [P, NT])
        den = pair("den", [P, NT])
        rden = pair("rden", [P, NT])
        top = pair("top", [P, NT, TOPK])
        stats = pair("stats", [P, NT, 6])
        mean_var = pair("mean_var", [P, NT, 2])
        var_eps = pair("var_eps", [P, NT])
        rstd = pair("rstd", [P, NT])
        has_edge = pair("has_edge", [P, NT])
        edge_nan = pair("edge_nan", [P, NT])
        den3 = pair("den3", [P, NT, NH])
        rden3 = pair("rden3", [P, NT, NH])

        def flat(bank):
            return bank[:].rearrange("p a b -> p (a b)")

        def chunks(ap):
            return ap.rearrange("p a b -> p (a b)").rearrange("p (c n) -> p c n", c=DC)

        q_hi = [chunks(R[s][:]) for s in range(SLOTS)]
        k_hi = [chunks(X[s][:]) for s in range(SLOTS)]
        q_lo = [chunks(HX[s][:]) for s in range(SLOTS)]
        k_lo = [chunks(neg1[s][:].bitcast(F32)) for s in range(SLOTS)]

        work = [[ctx.enter_context(nc.psum_tensor(f"work_{s}_{i}", [P, N], F32)) for i in range(2)]
                for s in range(SLOTS)]
        acc = [[ctx.enter_context(nc.psum_tensor(f"acc_{s}_{i}", [P, 2, D], F32)) for i in range(NT // 2)]
               for s in range(SLOTS)]

        loaded = sem("loaded")
        consts = sem("consts")
        folded = sem("folded")
        held = {engine: sem(f"held_{engine}") for engine in ("vector", "sync", "gpsimd")}
        x_in = signal("x_in", [("L0", 16)])
        adj_in = signal("adj_in", [("L0", 16)])
        sent = signal("sent", [("L3", 16)], first=16)
        masked = signal("masked", [("L0", 3)])

        uses = []
        for k in ATT:
            uses += [(f"xT {k}", DC), (f"s {k}", 1) if k in L1K else (f"v {k}", NT), (f"bc {k}", 1), (f"pT {k}", NT)]
            if k in L1K:
                uses += [(f"hT {k}", DC), (f"g {k}", FC)]
        uses += [("xT L3", DC), ("v L3", NT), ("q L3", DC), ("k L3", DC)]
        for k, stage in [(0, "scores"), (1, "scores"), (0, "pT")] + [
                q for h in range(2, NH) for q in ((h, "scores"), (h - 1, "pT"))] + [(NH - 1, "pT")]:
            uses.append((f"{stage} {HEADS[k]}", NT))
        uses += [("rdenT L3", 2), ("rden L3", DC)]
        turn = Events(None, uses)
        assert turn.per_batch % 2 == 0
        per_bank = turn.per_batch // 2
        filled = [[sem(f"filled_{s}_{i}") for i in range(2)] for s in range(SLOTS)]
        evacuated = [[sem(f"evacuated_{s}_{i}") for i in range(2)] for s in range(SLOTS)]

        acc_uses = [("L0", 1)] + [(k + c, 1) for k in L1K for c in ("", " ffn")] + [("L2", 1), ("heads", 1), ("L3", 1)]
        acc_filled = signal("acc_filled", acc_uses)
        acc_evacuated = signal("acc_evacuated", acc_uses, first=1)

        neg_z_ready = signal("neg_z_ready", [(k, 1) for k in ATT])
        neg_max_ready = signal("neg_max_ready", [(k, 1) for k in ATT + HEADS])
        edge_step = signal("edge_step", [("L0", 3)])
        topk_step = signal("topk_step", [("L2", 3 * NT)])
        alpha_target_ready = signal("alpha_target_ready", [(k, 1) for k in ATT])
        alpha_z_done = signal("alpha_z_done", [(k, NT) for k in ATT])
        lrelu_done = signal("lrelu_done", [(k, NT) for k in ATT])
        exp_done = signal("exp_done", [(k, NT) for k in ATT + HEADS])
        split = signal("split", [("L3", 2 * DC)])
        stacked = [signal(f"stacked{i}", [(k, 8 * 16) for k in HEADS[i::2]]) for i in range(2)]
        kept = signal("kept", [("L2", NT)])
        rden_ready = signal("rden_ready", [(k, 1) for k in ATT + ["L3"]])
        elu_step = signal("elu_step", [("L0", 2), ("L2", 2)])
        sum_ready = signal("sum_ready", [(k, 1) for k in ("L0", "L1", "L2")])
        norms = [(k, 1) for k in ["L0"] + [q + c for q in L1K for c in (" h", " x")] + ["L1", "L2", "L3"]]
        stats_ready = signal("stats_ready", norms)
        mean_ready = signal("mean_ready", norms)
        var_ready = signal("var_ready", norms)
        rstd_ready = signal("rstd_ready", norms)
        normed = signal("normed", norms)
        affine_half = signal("affine_half", [(k + c, 1) for k in L1K for c in (" h", " x")])
        affine_done = signal("affine_done", [(k + c, 1) for k in L1K for c in (" h", " x")])

        def hold(eng, name="vector"):
            eng.sem_inc(held[name], 1)

        class Use:

            def __init__(self, s, it, key, n=0):
                i = turn.index(key, n)
                self.bank = work[s][i % 2]
                self.filled, self.evacuated = filled[s][i % 2], evacuated[s][i % 2]
                self.turn = it.times(per_bank, i // 2 + 1)

        def target_score(s, key, t):
            return s12[s][:, t, 0:1] if key in L1K else V[s][:, t, D:D + 1]

        def weights(s, key):
            return PT[s] if key in HEADS and HEADS.index(key) % 2 else T[s]

        def transposed(s, key):
            return PT2[:, HEADS.index(key) % 2] if key in HEADS else PT[s]

        SOURCE = {"L0": HX, "L1.0": X1, "L1.1": X, "L1.2": X, "L2": X1, "L3": X1}

        def wait_source(eng, s, it, key):
            if key == "L0":
                eng.wait_ge(x_in.sems[s], x_in.value(it, "L0", 15))
            elif key in ("L1.1", "L1.2"):
                eng.wait_ge(affine_done.sems[s], affine_done.value(it, L1K[L1K.index(key) - 1] + " x"))
            else:
                eng.wait_ge(normed.sems[s], normed.value(it, {"L1.0": "L0", "L2": "L1", "L3": "L2"}[key]))

        def walk(it, order, stages):
            for s, ahead, stage, key in order:
                if stage in stages:
                    stages[stage](s, Batch(it, ahead), key)

        N_LOADS = 6 + L * (2 * DC + 5 + 5) + 4
        N_CONSTS = 8
        N_FOLDED = 4 * DC + 2 * L + 1

        block = ctx.enter_context(nc.Block())

        @block.sync
        def _(sp):
            n_loads = [0]

            def load(dst, src):
                sp.dma_start(dst, src).then_inc(loaded, 16)
                n_loads[0] += 1

            def load_columns(dst, src):
                sp.dma_start(dst, src.rearrange("(c p) -> p c", p=P), allow_slow_non_contiguous=True)\
                    .then_inc(loaded, 16)
                n_loads[0] += 1

            def load_x(s, it):
                sp.dma_start(HX[s][:], x[it.times(SLOTS, s)].rearrange("(t p) d -> p t d", p=P)).then_inc(x_in.sems[s], 16)

            def row(src):
                return src.rearrange("(o d) one -> o (d one)", o=1)

            for s in range(SLOTS):
                sp.sem_inc(sent.sems[s], 16)
            load_x(0, Batch(0, 0))
            load_x(1, Batch(0, 0))
            load(w0_sb[:, :, 0:D], w0.rearrange("(c p) n -> p c n", p=P))
            load(PT2[:, 0, 0, 0:D], row(a01).broadcast_to([P, D]))
            load(PT2[:, 0, 1, 0:D], row(a02).broadcast_to([P, D]))
            load(PT2[:, 0, 2, 0:2 * D], row(a2g).broadcast_to([P, 2 * D]))
            load(PT2[:, 0, 3, 0:L], attn_b.rearrange("(o l) -> o l", o=1).broadcast_to([P, L]))
            load(wg_sb[:, :, 0:D], w2g.rearrange("(c p) n -> p c n", p=P))
            for l in range(L):
                for half in range(2):
                    for c in range(DC):
                        load(aw_sb[:, l, c, half:half + 1],
                             attn_w[l, half * D + c * P:half * D + (c + 1) * P].rearrange("(p one) -> p one", one=1))
                load(w1_sb[:, l], w1[l].rearrange("(c p) f -> p c f", p=P))
                load(w2_sb[:, l], w2[l].rearrange("(c p) n -> p c n", p=P))
                load_columns(b1_sb[:, l], b1[l])
                load_columns(g1t_sb[:, l], g1[l])
                load_columns(beta1t_sb[:, l], beta1[l])
                for dst, src in ((g1_sb[:, l], g1), (c1_sb[:, l], beta1), (PT2[:, 1, l, 0:D], b2),
                                 (g2_sb[:, l], g2), (beta2_sb[:, l], beta2)):
                    load(dst, src[l:l + 1, :].broadcast_to([P, D]))
            for dst, src in ((wq_sb, wq), (wk_sb, wk), (wv_sb, wv), (wo_sb, wo)):
                load(dst[:], src.rearrange("(c p) n -> p c n", p=P))
            assert n_loads[0] == N_LOADS

            def load_next(s, it, key):
                if it.is_number(PAIRS - 1):
                    return
                sp.wait_ge(stacked[1].sems[s], stacked[1].value(it, HEADS[-1], 8 * 16 - 1))
                hold(sp, "sync")
                load_x(s, it.next())

            def stack(s, it, key):
                h = HEADS.index(key)
                m, r = h // HPC, h % HPC * DK
                if h == 0:
                    u = Use(s, it, "k L3", 0)
                    sp.wait_ge(u.evacuated, u.turn + 1)
                    hold(sp, "sync")
                    u = Use(s, it, "k L3", 1)
                    sp.wait_ge(u.evacuated, u.turn + 1)
                    hold(sp, "sync")
                elif h > 1:
                    u = Use(s, it, f"scores {HEADS[h - 2]}", NT - 1)
                    sp.wait_ge(u.filled, u.turn)
                    hold(sp, "sync")
                for row, (q_half, k_half) in enumerate(((q_hi, k_hi), (q_hi, k_lo), (q_lo, k_hi), (q_lo, k_lo))):
                    for dst, src in ((q4, q_half), (k4, k_half)):
                        sp.dma_start(dst[row * DK:(row + 1) * DK, h % 2, :].bitcast(F32), src[s][r:r + DK, m, :])\
                            .then_inc(stacked[h % 2].sems[s], 16)

            def store(s, it, key):
                sp.wait_ge(normed.sems[s], normed.value(it, "L3"))
                hold(sp, "sync")
                sp.dma_start(out[it.times(SLOTS, s)].rearrange("(t p) d -> p t d", p=P), X[s][:]).then_inc(sent.sems[s], 16)

            stages = {"load": load_next, "stack": stack, "store": store}
            walk(0, opening, stages)
            with sp.Fori(0, PAIRS - 1) as it:
                walk(it, to_a, stages)
                walk(it + 1, to_b, stages)
            walk(PAIRS - 1, closing, stages)
            for s in range(SLOTS):
                sp.wait_ge(sent.sems[s], sent.value(Batch(PAIRS - 1, 0), "L3", 15))

        @block.gpsimd
        def _(pool):
            def load_adj(s, it):
                pool.dma_start(neg1[s][:], adj[it.times(SLOTS, s)].rearrange("(t p) j -> p t j", p=P))\
                    .then_inc(adj_in.sems[s], 16)

            for s in range(SLOTS):
                load_adj(s, Batch(0, 0))
            pool.memset(ident[:], 0.0).then_inc(consts, 1)
            pool.memset(no_diag[:], 1.0).then_inc(consts, 1)
            pool.memset(minus_half[:], -0.5).then_inc(consts, 1)
            pool.memset(head_rows[:], 1.0).then_inc(consts, 1)
            pool.wait_ge(consts, 4)
            for m, fill_with in ((ident, 1.0), (no_diag, 0.0)):
                pool.affine_select(out=m[:], in_=m[:], compare_op=ALU.not_equal, fill=fill_with, base=0,
                                   pattern=[[-1, P]], channel_multiplier=1).then_inc(consts, 1)
            features = [[P, DC], [1, P]]
            pool.affine_select(out=head_rows[:], in_=head_rows[:], compare_op=ALU.is_ge, fill=0.0, base=0,
                               pattern=features, channel_multiplier=-DK).then_inc(consts, 1)
            pool.wait_ge(consts, N_CONSTS - 1)
            pool.affine_select(out=head_rows[:], in_=head_rows[:], compare_op=ALU.is_ge, fill=0.0, base=DK - 1,
                               pattern=[[-P, DC], [-1, P]], channel_multiplier=DK).then_inc(consts, 1)
            pool.wait_ge(consts, N_CONSTS)
            pool.wait_ge(folded, N_FOLDED)

            def rsqrt(s, it, key):
                pool.wait_ge(var_ready.sems[s], var_ready.value(it, key))
                pool.tensor_tensor(rstd[s][:], var_eps[s][:], minus_half[:], ALU.pow).then_inc(rstd_ready.sems[s], 1)

            def affine(s, it, key, dst, src, gain, shift):
                l = L1K.index(key[:4])
                pool.wait_ge(normed.sems[s], normed.value(it, key))
                pool.tensor_tensor(dst[:], src[:], gain[:, l:l + 1, :].broadcast_to([P, NT, D]), ALU.mult)\
                    .then_inc(affine_half.sems[s], 1)
                pool.wait_ge(affine_half.sems[s], affine_half.value(it, key))
                pool.tensor_tensor(dst[:], dst[:], shift[:, l:l + 1, :].broadcast_to([P, NT, D]), ALU.add)\
                    .then_inc(affine_done.sems[s], 1)

            def after_sum(s, it, key):
                rsqrt(s, it, key + " h" if key in L1K else key)

            def h_affine(s, it, key):
                if key in L1K:
                    affine(s, it, key + " h", R[s], HX[s], g1_sb, c1_sb)

            def after_xsum(s, it, key):
                rsqrt(s, it, key + " x")

            def x_affine(s, it, key):
                affine(s, it, key + " x", X[s], X[s], g2_sb, beta2_sb)

            def after_l1sum(s, it, key):
                rsqrt(s, it, "L1")

            def load_next(s, it, key):
                if it.is_number(PAIRS - 1):
                    return
                pool.wait_ge(stacked[1].sems[s], stacked[1].value(it, HEADS[-1], 8 * 16 - 1))
                hold(pool, "gpsimd")
                load_adj(s, it.next())

            stages = {"load": load_next, "sum": after_sum, "norm": h_affine, "xsum": after_xsum, "xnorm": x_affine,
                      "l1sum": after_l1sum, "ysum": rsqrt}
            walk(0, opening, stages)
            with pool.Fori(0, PAIRS - 1) as it:
                walk(it, to_a, stages)
                walk(it + 1, to_b, stages)
            walk(PAIRS - 1, closing, stages)

        @block.vector
        def _(dve):
            dve.wait_ge(loaded, 16 * N_LOADS)
            for c in range(DC):
                for half in range(2):
                    dve.tensor_tensor_reduce(X1[half][:, c, :], w0_sb[:, c, 0:D], PT2[:, 0, half, 0:D], 1.0, 0.0,
                                             ALU.mult, ALU.add, w0_sb[:, c, D + half:D + half + 1]).then_inc(folded, 1)
                    dve.tensor_tensor_reduce(X1[half][:, DC + c, :], wg_sb[:, c, 0:D], PT2[:, 0, 2, half * D:(half + 1) * D],
                                             1.0, 0.0, ALU.mult, ALU.add,
                                             wg_sb[:, c, D + half:D + half + 1]).then_inc(folded, 1)
            for l in range(L):
                dve.tensor_tensor(c1_sb[:, l], c1_sb[:, l], PT2[:, 1, l, 0:D], ALU.add).then_inc(folded, 1)
            dve.memset(ab_sb[:], 0.0).then_inc(folded, 1)
            dve.wait_ge(folded, 4 * DC + L + 1)
            for l in range(L):
                dve.tensor_copy(ab_sb[:, l, :, 0], PT2[:, 0, 3, l:l + 1].broadcast_to([P, NT])).then_inc(folded, 1)
            dve.wait_ge(folded, N_FOLDED)
            dve.wait_ge(consts, N_CONSTS)
            for s in range(SLOTS):
                dve.memset(den[s][:], 0.0).then_inc(evacuated[s][0], 1)
                dve.memset(rden[s][:], 0.0).then_inc(evacuated[s][1], 1)
                dve.memset(neg_z[s][:], 0.0).then_inc(acc_evacuated.sems[s], 1)

            def make_masks(s, it, key):
                dve.wait_ge(adj_in.sems[s], adj_in.value(it, "L0", 15))
                dve.tensor_scalar(neg0[s][:], neg1[s][:], 0.0, MASKED, ALU.is_equal, ALU.mult).then_inc(masked.sems[s], 1)
                dve.wait_ge(masked.sems[s], masked.value(it, "L0", 0))
                dve.tensor_copy(neg1[s][:], neg0[s][:]).then_inc(masked.sems[s], 1)
                dve.wait_ge(masked.sems[s], masked.value(it, "L0", 1))
                for t in range(NT):
                    last = dve.tensor_tensor(neg1[s][:, t, t * P:(t + 1) * P], neg0[s][:, t, t * P:(t + 1) * P],
                                             no_diag[:], ALU.mult)
                last.then_inc(masked.sems[s], 1)
                dve.wait_ge(masked.sems[s], masked.value(it, "L0", 2))

            def x_transposed(s, it, key):
                u = Use(s, it, f"xT {key}", 1)
                dve.wait_ge(u.filled, u.turn)
                dve.tensor_copy(XT[s][:, 1, :], u.bank[:]).then_inc(u.evacuated, 1)

            def scores_of_x(s, it, key):
                u = Use(s, it, f"s {key}")
                dve.wait_ge(u.filled, u.turn)
                dve.tensor_tensor(s12[s][:], u.bank[:, 0:NT * 2].rearrange("p (t k) -> p t k", k=2),
                                  ab_sb[:, L1K.index(key)], ALU.add).then_inc(u.evacuated, 1)

            def masked_max(s, it, key):
                u = Use(s, it, f"bc {key}")
                dve.wait_ge(u.filled, u.turn)
                neg = neg1 if key in L1K else neg0
                hold(dve)
                for t in range(NT):
                    last = dve.tensor_tensor_reduce(T[s][:, t, :], u.bank[:], neg[s][:, t, :], 1.0, LOWEST,
                                                    ALU.add, ALU.max, row_max[s][:, t:t + 1])
                last.then_inc(u.evacuated, 1)
                u = Use(s, it, f"bc {key}")
                dve.wait_ge(u.evacuated, u.turn + 1)
                target = s12[s][:, :, 0] if key in L1K else V[s][:, :, D]
                dve.scalar_tensor_tensor(neg_z[s][:], row_max[s][:], -1.0, target, ALU.mult, ALU.subtract)\
                    .then_inc(neg_z_ready.sems[s], 1)
                if key == "L0":
                    dve.tensor_scalar(has_edge[s][:], row_max[s][:], 0.5 * MASKED, None, ALU.is_gt)\
                        .then_inc(edge_step.sems[s], 1)
                    dve.wait_ge(edge_step.sems[s], edge_step.value(it, "L0", 0))
                    dve.reciprocal(edge_nan[s][:], has_edge[s][:]).then_inc(edge_step.sems[s], 1)
                    dve.wait_ge(edge_step.sems[s], edge_step.value(it, "L0", 1))
                    dve.tensor_tensor(edge_nan[s][:], edge_nan[s][:], has_edge[s][:], ALU.mult)\
                        .then_inc(edge_step.sems[s], 1)
                dve.tensor_scalar(alpha_target[s][:], target, ALPHA[key], None, ALU.mult)\
                    .then_inc(alpha_target_ready.sems[s], 1)
                dve.wait_ge(neg_z_ready.sems[s], neg_z_ready.value(it, key))
                dve.scalar_tensor_tensor(neg_max[s][:], neg_z[s][:], ALPHA[key], neg_z[s][:], ALU.mult, ALU.min)\
                    .then_inc(neg_max_ready.sems[s], 1)

            def topk(s, it, key):
                for t in range(NT):
                    dve.max(top[s][:, t, 0:8], T[s][:, t, :]).then_inc(topk_step.sems[s], 1)
                for t in range(NT):
                    dve.wait_ge(topk_step.sems[s], topk_step.value(it, "L2", t))
                    hold(dve)
                    dve.match_replace(PT[s][:, t, :], top[s][:, t, 0:8], T[s][:, t, :], LOWEST)\
                        .then_inc(topk_step.sems[s], 1)
                for t in range(NT):
                    dve.wait_ge(topk_step.sems[s], topk_step.value(it, "L2", NT + t))
                    hold(dve)
                    dve.max(top[s][:, t, 8:16], PT[s][:, t, :]).then_inc(topk_step.sems[s], 1)

            def lrelu(s, it, key):
                for t in range(NT):
                    dve.wait_ge(alpha_z_done.sems[s], alpha_z_done.value(it, key, t))
                    dve.scalar_tensor_tensor(PT[s][:, t, :], T[s][:, t, :], target_score(s, key, t), PT[s][:, t, :],
                                             ALU.add, ALU.max).then_inc(lrelu_done.sems[s], 1)

            def weights_transposed(s, it, key):
                if key == "L2":
                    dve.wait_ge(topk_step.sems[s], topk_step.value(it, "L2", 3 * NT - 1))
                    for t in range(NT):
                        dve.wait_ge(exp_done.sems[s], exp_done.value(it, key, t))
                        dve.scalar_tensor_tensor(T[s][:, t, :], T[s][:, t, :], top[s][:, t, TOPK - 1:TOPK],
                                                 PT[s][:, t, :], ALU.is_ge, ALU.mult).then_inc(kept.sems[s], 1)
                if key in ATT:
                    dve.wait_ge(exp_done.sems[s], exp_done.value(it, key, NT - 1))
                    dve.reciprocal(rden[s][:], den[s][:]).then_inc(rden_ready.sems[s], 1)
                dst = transposed(s, key)
                for j in range(1, NT, 2):
                    u = Use(s, it, f"pT {key}", j)
                    dve.wait_ge(u.filled, u.turn)
                    dve.tensor_copy(dst[:, j, :], u.bank[:]).then_inc(u.evacuated, 1)

            def statistics(s, it, key):
                for t in range(NT):
                    last = dve.bn_stats(stats[s][:, t, :], R[s][:, t, :])
                last.then_inc(stats_ready.sems[s], 1)
                dve.wait_ge(stats_ready.sems[s], stats_ready.value(it, key))
                hold(dve)
                for t in range(NT):
                    last = dve.bn_aggr(mean_var[s][:, t, :], stats[s][:, t, :])
                last.then_inc(mean_ready.sems[s], 1)
                dve.wait_ge(mean_ready.sems[s], mean_ready.value(it, key))
                dve.tensor_scalar(var_eps[s][:], mean_var[s][:, :, 1], EPS, None, ALU.add).then_inc(var_ready.sems[s], 1)

            def normalize(s, it, key, dst):
                dve.wait_ge(rstd_ready.sems[s], rstd_ready.value(it, key))
                for t in range(NT):
                    last = dve.tensor_scalar(dst[:, t, :], R[s][:, t, :], mean_var[s][:, t, 0:1], rstd[s][:, t:t + 1],
                                             ALU.subtract, ALU.mult)
                last.then_inc(normed.sems[s], 1)

            def aggregated(s, it, key):
                if key in L1K:
                    wait_source(dve, s, it, key)
                    dve.wait_ge(rden_ready.sems[s], rden_ready.value(it, key))
                    dve.wait_ge(acc_filled.sems[s], acc_filled.value(it, key))
                    for t in range(NT):
                        last = dve.scalar_tensor_tensor(R[s][:, t, :], acc[s][t // 2][:, t % 2, :], rden[s][:, t:t + 1],
                                                        SOURCE[key][s][:, t, :], ALU.mult, ALU.add)
                    last.then_inc(acc_evacuated.sems[s], 1)
                    dve.wait_ge(acc_evacuated.sems[s], acc_evacuated.value(it, key))
                    statistics(s, it, key + " h")
                else:
                    E = T[s][:, :, 0:D]
                    dve.wait_ge(acc_evacuated.sems[s], acc_evacuated.value(it, key))
                    dve.tensor_scalar(E, E, 1.0, -1.0, ALU.min, ALU.add).then_inc(elu_step.sems[s], 1)
                    dve.wait_ge(elu_step.sems[s], elu_step.value(it, key, 0))
                    dve.tensor_tensor(R[s][:], R[s][:], E, ALU.max).then_inc(elu_step.sems[s], 1)
                    dve.wait_ge(elu_step.sems[s], elu_step.value(it, key, 1))
                    dve.tensor_tensor(R[s][:], R[s][:], SOURCE[key][s][:], ALU.add).then_inc(sum_ready.sems[s], 1)
                    dve.wait_ge(sum_ready.sems[s], sum_ready.value(it, key))
                    statistics(s, it, key)

            def norm(s, it, key):
                if key in L1K:
                    normalize(s, it, key + " h", HX[s])
                elif key == "L3":
                    normalize(s, it, key, X[s])
                else:
                    normalize(s, it, key, X1[s])

            def h_transposed(s, it, key):
                l = L1K.index(key)
                u = Use(s, it, f"hT {key}", 1)
                dve.wait_ge(u.filled, u.turn)
                dve.tensor_scalar(XT[s][:, 1, :], u.bank[:], g1t_sb[:, l, 1:2], beta1t_sb[:, l, 1:2], ALU.mult, ALU.add)\
                    .then_inc(u.evacuated, 1)

            def after_ffn(s, it, key):
                dve.wait_ge(affine_done.sems[s], affine_done.value(it, key + " h"))
                dve.wait_ge(acc_filled.sems[s], acc_filled.value(it, key + " ffn"))
                for i in range(NT // 2):
                    last = dve.tensor_tensor(R[s][:, 2 * i:2 * i + 2, :], acc[s][i][:], R[s][:, 2 * i:2 * i + 2, :],
                                             ALU.add)
                last.then_inc(acc_evacuated.sems[s], 1)
                dve.wait_ge(acc_evacuated.sems[s], acc_evacuated.value(it, key + " ffn"))
                statistics(s, it, key + " x")

            def x_norm(s, it, key):
                if key == L1K[0]:
                    dve.wait_ge(sent.sems[s], it.times(16, 16))
                normalize(s, it, key + " x", X[s])

            def l1_sum(s, it, key):
                dve.wait_ge(affine_done.sems[s], affine_done.value(it, L1K[-1] + " x"))
                dve.tensor_tensor(R[s][:], X[s][:], X1[s][:], ALU.add).then_inc(sum_ready.sems[s], 1)
                dve.wait_ge(sum_ready.sems[s], sum_ready.value(it, "L1"))
                statistics(s, it, "L1")

            def qkv(s, it, key):
                for i, (name, hi, lo, scale) in enumerate((("q L3", q_hi, q_lo, float(DK) ** -0.5), ("k L3", k_hi, k_lo, 1.0))):
                    for c in range(DC):
                        u = Use(s, it, name, c)
                        dve.wait_ge(split.sems[s], split.value(it, "L3", i * DC + c))
                        dve.scalar_tensor_tensor(lo[s][:, c, :].bitcast(F32R), u.bank[:], scale, hi[s][:, c, :],
                                                 ALU.mult, ALU.subtract).then_inc(u.evacuated, 1)

            def head_scores(s, it, key):
                dst = weights(s, key)
                h = HEADS.index(key)
                if h:
                    dve.wait_ge(neg_max_ready.sems[s], neg_max_ready.value(it, HEADS[h - 1]))
                for t in range(NT):
                    u = Use(s, it, f"scores {key}", t)
                    dve.wait_ge(u.filled, u.turn)
                    hold(dve)
                    dve.tensor_tensor_reduce(dst[:, t, :], u.bank[:], neg0[s][:, t, :], 1.0, LOWEST, ALU.add, ALU.max,
                                             row_max[s][:, t:t + 1]).then_inc(u.evacuated, 1)
                if h:
                    dve.wait_ge(exp_done.sems[s], exp_done.value(it, HEADS[h - 1], NT - 1))
                u = Use(s, it, f"scores {key}", NT - 2)
                dve.wait_ge(u.evacuated, u.turn + 1)
                u = Use(s, it, f"scores {key}", NT - 1)
                dve.wait_ge(u.evacuated, u.turn + 1)
                dve.tensor_scalar(neg_max[s][:], row_max[s][:], -1.0, None, ALU.mult).then_inc(neg_max_ready.sems[s], 1)

            def heads_normed(s, it, key):
                dve.wait_ge(exp_done.sems[s], exp_done.value(it, HEADS[-1], NT - 1))
                dve.reciprocal(rden3[s][:], den3[s][:]).then_inc(rden_ready.sems[s], 1)
                dve.wait_ge(acc_filled.sems[s], acc_filled.value(it, "heads"))
                for m in range(DC):
                    u = Use(s, it, "rden L3", m)
                    dve.wait_ge(u.evacuated, u.turn + 1)
                    last = dve.scalar_tensor_tensor(XT[s][:, m, :], flat(acc[s][m]), 0.0, chunks(R[s][:])[:, m, :],
                                                    ALU.max, ALU.mult)
                last.then_inc(acc_evacuated.sems[s], 1)

            def after_proj(s, it, key):
                dve.wait_ge(acc_filled.sems[s], acc_filled.value(it, "L3"))
                for t in range(NT):
                    last = dve.scalar_tensor_tensor(R[s][:, t, :], X1[s][:, t, :], edge_nan[s][:, t:t + 1],
                                                    acc[s][t // 2][:, t % 2, :], ALU.mult, ALU.add)
                last.then_inc(acc_evacuated.sems[s], 1)
                dve.wait_ge(acc_evacuated.sems[s], acc_evacuated.value(it, "L3"))
                statistics(s, it, "L3")

            stages = {"masks": make_masks, "xT": x_transposed, "s": scores_of_x, "bc": masked_max, "topk": topk,
                      "lrelu": lrelu, "pT": weights_transposed, "sum": aggregated, "norm": norm, "hT": h_transposed,
                      "xsum": after_ffn, "xnorm": x_norm, "l1sum": l1_sum, "qkv": qkv, "scores": head_scores,
                      "heads": heads_normed, "ysum": after_proj}
            walk(0, opening, stages)
            with dve.Fori(0, PAIRS - 1) as it:
                walk(it, to_a, stages)
                walk(it + 1, to_b, stages)
            walk(PAIRS - 1, closing, stages)

        @block.scalar
        def _(act):
            act.wait_ge(loaded, 16 * N_LOADS)
            act.wait_ge(folded, N_FOLDED)

            def x_transposed(s, it, key):
                u = Use(s, it, f"xT {key}", 0)
                act.wait_ge(u.filled, u.turn)
                act.activation(XT[s][:, 0, :], u.bank[:], ACT.Copy).then_inc(u.evacuated, 1)

            def projected(s, it, key):
                for t in range(NT):
                    u = Use(s, it, f"v {key}", t)
                    act.wait_ge(u.filled, u.turn)
                    act.activation(V[s][:, t, :], u.bank[:, 0:DA], ACT.Copy).then_inc(u.evacuated, 1)

            def alpha_z(s, it, key):
                if key == "L2":
                    act.wait_ge(topk_step.sems[s], topk_step.value(it, "L2", 3 * NT - 1))
                act.wait_ge(alpha_target_ready.sems[s], alpha_target_ready.value(it, key))
                for t in range(NT):
                    act.activation(PT[s][:, t, :], T[s][:, t, :], ACT.Identity, bias=alpha_target[s][:, t:t + 1],
                                   scale=ALPHA[key]).then_inc(alpha_z_done.sems[s], 1)

            def exp(s, it, key):
                if key in HEADS:
                    act.wait_ge(neg_max_ready.sems[s], neg_max_ready.value(it, key))
                    h = HEADS.index(key)
                    z = weights(s, key)
                    for t in range(NT):
                        act.activation(z[:, t, :], z[:, t, :], ACT.Exp, bias=neg_max[s][:, t:t + 1],
                                       accum_out=den3[s][:, t, h:h + 1]).then_inc(exp_done.sems[s], 1)
                    return
                dst = PT if key == "L2" else T
                for t in range(NT):
                    act.wait_ge(lrelu_done.sems[s], lrelu_done.value(it, key, t))
                    act.activation(dst[s][:, t, :], PT[s][:, t, :], ACT.Exp, bias=neg_max[s][:, t:t + 1],
                                   accum_out=den[s][:, t:t + 1]).then_inc(exp_done.sems[s], 1)

            def weights_transposed(s, it, key):
                dst = transposed(s, key)
                for j in range(0, NT, 2):
                    u = Use(s, it, f"pT {key}", j)
                    act.wait_ge(u.filled, u.turn)
                    act.activation(dst[:, j, :], u.bank[:], ACT.Copy).then_inc(u.evacuated, 1)

            def agg(s, it, key):
                if key in L1K:
                    return
                act.wait_ge(rden_ready.sems[s], rden_ready.value(it, key))
                act.wait_ge(acc_filled.sems[s], acc_filled.value(it, key))
                for t in range(NT):
                    act.activation(R[s][:, t, :], acc[s][t // 2][:, t % 2, :], ACT.Copy, scale=rden[s][:, t:t + 1])
                for t in range(NT):
                    last = act.activation(T[s][:, t, 0:D], acc[s][t // 2][:, t % 2, :], ACT.Exp,
                                          scale=rden[s][:, t:t + 1])
                last.then_inc(acc_evacuated.sems[s], 1)

            def h_transposed(s, it, key):
                l = L1K.index(key)
                u = Use(s, it, f"hT {key}", 0)
                act.wait_ge(u.filled, u.turn)
                act.activation(XT[s][:, 0, :], u.bank[:], ACT.Identity, scale=g1t_sb[:, l, 0:1],
                               bias=beta1t_sb[:, l, 0:1]).then_inc(u.evacuated, 1)

            def gelu(quarter):
                def stage(s, it, key):
                    l = L1K.index(key)
                    for f in range(quarter * FC // 4, (quarter + 1) * FC // 4):
                        u = Use(s, it, f"g {key}", f)
                        act.wait_ge(u.filled, u.turn)
                        act.activation(gT[:, f % (FC // 2), :], u.bank[:], ACT.Gelu, bias=b1_sb[:, l, f:f + 1]).then_inc(u.evacuated, 1)
                return stage

            def qkv(s, it, key):
                for t in range(NT):
                    u = Use(s, it, "v L3", t)
                    act.wait_ge(u.filled, u.turn)
                    act.activation(V[s][:, t, 0:D], u.bank[:, 0:D], ACT.Copy).then_inc(u.evacuated, 1)
                for name, hi, scale in (("q L3", q_hi, float(DK) ** -0.5), ("k L3", k_hi, 1.0)):
                    for c in range(DC):
                        u = Use(s, it, name, c)
                        act.wait_ge(u.filled, u.turn)
                        act.activation(hi[s][:, c, :].bitcast(F32R), u.bank[:], ACT.Copy, scale=scale)\
                            .then_inc(split.sems[s], 1)

            def heads_rden(s, it, key):
                for i in range(2):
                    u = Use(s, it, "rdenT L3", i)
                    act.wait_ge(u.filled, u.turn)
                    act.activation(T[s][0:NH, 0, i * N // 2:(i + 1) * N // 2], u.bank[0:NH, 0:N // 2], ACT.Copy)\
                        .then_inc(u.evacuated, 1)
                for m in range(DC):
                    u = Use(s, it, "rden L3", m)
                    act.wait_ge(u.filled, u.turn)
                    act.activation(chunks(R[s][:])[:, m, :], u.bank[:], ACT.Copy).then_inc(u.evacuated, 1)

            stages = {"xT": x_transposed, "v": projected, "alphaz": alpha_z, "exp": exp, "pT": weights_transposed,
                      "agg": agg, "hT": h_transposed, "ffn1a": gelu(0), "ffn1b": gelu(1), "ffn1c": gelu(2), "ffn1d": gelu(3),
                      "qkv": qkv, "heads": heads_rden}
            walk(0, opening, stages)
            with act.Fori(0, PAIRS - 1) as it:
                walk(it, to_a, stages)
                walk(it + 1, to_b, stages)
            walk(PAIRS - 1, closing, stages)

        @block.tensor
        def _(pe):
            pe.wait_ge(loaded, 16 * N_LOADS)
            pe.wait_ge(consts, N_CONSTS)
            pe.wait_ge(folded, N_FOLDED)

            def transpose_tiles(s, it, key, n, src, c):
                u = Use(s, it, key, n)
                pe.wait_ge(u.evacuated, u.turn)
                for t in range(NT):
                    last = pe.transpose(u.bank[:, t * P:(t + 1) * P], src[:, t, c * P:(c + 1) * P], ident[:])
                last.then_inc(u.filled, 1)

            def xT(s, it, key):
                wait_source(pe, s, it, key)
                for c in range(DC):
                    transpose_tiles(s, it, f"xT {key}", c, SOURCE[key][s], c)

            def project(s, it, key, weights, columns):
                for t in range(NT):
                    u = Use(s, it, key, t)
                    pe.wait_ge(u.evacuated, u.turn)
                    for c in range(DC):
                        last = pe.matmul(u.bank[:, 0:columns], XT[s][:, c, t * P:(t + 1) * P], weights[:, c, 0:columns],
                                         start=(c == 0), stop=(c == DC - 1))
                    last.then_inc(u.filled, 1)

            def project_v(s, it, key):
                for c in range(DC):
                    u = Use(s, it, f"xT {key}", c)
                    pe.wait_ge(u.evacuated, u.turn + 1)
                project(s, it, f"v {key}", w0_sb if key == "L0" else wg_sb, DA)

            def scores_of_x(s, it, key):
                for c in range(DC):
                    u = Use(s, it, f"xT {key}", c)
                    pe.wait_ge(u.evacuated, u.turn + 1)
                u = Use(s, it, f"s {key}")
                pe.wait_ge(u.evacuated, u.turn)
                for t in range(NT):
                    for c in range(DC):
                        last = pe.matmul(u.bank[:, 2 * t:2 * t + 2], XT[s][:, c, t * P:(t + 1) * P],
                                         aw_sb[:, L1K.index(key), c, :], start=(c == 0), stop=(c == DC - 1))
                last.then_inc(u.filled, 1)

            def broadcast(s, it, key):
                if key in L1K:
                    u = Use(s, it, f"s {key}")
                    pe.wait_ge(u.evacuated, u.turn + 1)
                else:
                    for t in range(NT - 2, NT):
                        u = Use(s, it, f"v {key}", t)
                        pe.wait_ge(u.evacuated, u.turn + 1)
                u = Use(s, it, f"bc {key}")
                pe.wait_ge(u.evacuated, u.turn)
                for t in range(NT):
                    col = s12[s][:, t, 1:2] if key in L1K else V[s][:, t, D + 1:D + 2]
                    last = pe.transpose(u.bank[:, t * P:(t + 1) * P], col.broadcast_to([P, P]), ident[:])
                last.then_inc(u.filled, 1)

            def weights_transposed(s, it, key):
                if key == "L2":
                    pe.wait_ge(kept.sems[s], kept.value(it, key, NT - 1))
                else:
                    pe.wait_ge(exp_done.sems[s], exp_done.value(it, key, NT - 1))
                for j in range(NT):
                    transpose_tiles(s, it, f"pT {key}", j, weights(s, key), j)

            def agg(s, it, key):
                pe.wait_ge(acc_evacuated.sems[s], acc_evacuated.value(it, key) - 1)
                src = SOURCE[key] if key in L1K else V
                for j in range(NT):
                    u = Use(s, it, f"pT {key}", j)
                    pe.wait_ge(u.evacuated, u.turn + 1)
                    for t in range(NT):
                        last = pe.matmul(acc[s][t // 2][:, t % 2, :], PT[s][:, j, t * P:(t + 1) * P], src[s][:, j, 0:D],
                                         start=(j == 0 and t % 2 == 0), stop=(j == NT - 1), skip_group_check=True)
                last.then_inc(acc_filled.sems[s], 1)

            def h_transposed(s, it, key):
                pe.wait_ge(normed.sems[s], normed.value(it, key + " h"))
                for c in range(DC):
                    transpose_tiles(s, it, f"hT {key}", c, HX[s], c)

            def ffn1(quarter):
                def stage(s, it, key):
                    l = L1K.index(key)
                    for c in range(DC):
                        u = Use(s, it, f"hT {key}", c)
                        pe.wait_ge(u.evacuated, u.turn + 1)
                    for f in range(quarter * FC // 4, (quarter + 1) * FC // 4):
                        u = Use(s, it, f"g {key}", f)
                        pe.wait_ge(u.evacuated, u.turn)
                        for c in range(DC):
                            last = pe.matmul(u.bank[:], w1_sb[:, l, c, f * P:(f + 1) * P], XT[s][:, c, :],
                                             start=(c == 0), stop=(c == DC - 1))
                        last.then_inc(u.filled, 1)
                return stage

            def ffn2(quarter):
                def stage(s, it, key):
                    l = L1K.index(key)
                    if quarter == 0:
                        pe.wait_ge(acc_evacuated.sems[s], acc_evacuated.value(it, key + " ffn") - 1)
                    for f in range(quarter * FC // 4, (quarter + 1) * FC // 4):
                        u = Use(s, it, f"g {key}", f)
                        pe.wait_ge(u.evacuated, u.turn + 1)
                        for t in range(NT):
                            last = pe.matmul(acc[s][t // 2][:, t % 2, :], gT[:, f % (FC // 2), t * P:(t + 1) * P], w2_sb[:, l, f, :],
                                             start=(f == 0 and t % 2 == 0), stop=(f == FC - 1), skip_group_check=True)
                    if quarter == 3:
                        last.then_inc(acc_filled.sems[s], 1)
                return stage

            def qkv(s, it, key):
                for c in range(DC):
                    u = Use(s, it, "xT L3", c)
                    pe.wait_ge(u.evacuated, u.turn + 1)
                project(s, it, "v L3", wv_sb, D)
                for name, w in (("q L3", wq_sb), ("k L3", wk_sb)):
                    for m in range(DC):
                        u = Use(s, it, name, m)
                        pe.wait_ge(u.evacuated, u.turn)
                        for c in range(DC):
                            last = pe.matmul(u.bank[:], w[:, c, m * P:(m + 1) * P], XT[s][:, c, :],
                                             start=(c == 0), stop=(c == DC - 1))
                        last.then_inc(u.filled, 1)

            def head_scores(s, it, key):
                h = HEADS.index(key)
                pe.wait_ge(stacked[h % 2].sems[s], stacked[h % 2].value(it, key, 8 * 16 - 1))
                for t in range(NT):
                    u = Use(s, it, f"scores {key}", t)
                    pe.wait_ge(u.evacuated, u.turn)
                    pe.matmul(u.bank[:], q4[:, h % 2, t * P:(t + 1) * P], k4[:, h % 2, :],
                              start=True, stop=True).then_inc(u.filled, 1)

            def head_outputs(s, it, key):
                h = HEADS.index(key)
                if h == 1:
                    pe.wait_ge(acc_evacuated.sems[s], acc_evacuated.value(it, "heads") - 1)
                for j in range(NT):
                    u = Use(s, it, f"pT {key}", j)
                    pe.wait_ge(u.evacuated, u.turn + 1)
                    for hh in (h - 1, h):
                        m, r = hh // HPC, hh % HPC * DK
                        last = pe.matmul(flat(acc[s][m])[r:r + DK, :], V[s][:, j, hh * DK:(hh + 1) * DK], PT2[:, hh % 2, j, :],
                                         start=(j == 0), stop=(j == NT - 1), skip_group_check=True)
                if h == NH - 1:
                    last.then_inc(acc_filled.sems[s], 1)

            def heads_rden(s, it, key):
                pe.wait_ge(rden_ready.sems[s], rden_ready.value(it, "L3"))
                for i in range(2):
                    u = Use(s, it, "rdenT L3", i)
                    pe.wait_ge(u.evacuated, u.turn)
                    for t in range(NT // 2):
                        last = pe.transpose(u.bank[0:NH, t * P:(t + 1) * P], rden3[s][:, i * NT // 2 + t, :], ident[:])
                    last.then_inc(u.filled, 1)
                for i in range(2):
                    u = Use(s, it, "rdenT L3", i)
                    pe.wait_ge(u.evacuated, u.turn + 1)
                for m in range(DC):
                    u = Use(s, it, "rden L3", m)
                    pe.matmul(u.bank[:], head_rows[:, m, :], T[s][0:NH, 0, :], start=True, stop=True).then_inc(u.filled, 1)

            def proj(s, it, key):
                pe.wait_ge(acc_evacuated.sems[s], acc_evacuated.value(it, "L3") - 1)
                for t in range(NT):
                    for c in range(DC):
                        last = pe.matmul(acc[s][t // 2][:, t % 2, :], XT[s][:, c, t * P:(t + 1) * P], wo_sb[:, c, :],
                                         start=(c == 0 and t % 2 == 0), stop=(c == DC - 1), skip_group_check=True)
                last.then_inc(acc_filled.sems[s], 1)

            stages = {"xT": xT, "v": project_v, "s": scores_of_x, "bc": broadcast, "pT": weights_transposed, "agg": agg,
                      "hT": h_transposed, "ffn1a": ffn1(0), "ffn1b": ffn1(1), "ffn1c": ffn1(2), "ffn1d": ffn1(3),
                      "ffn2a": ffn2(0), "ffn2b": ffn2(1), "ffn2c": ffn2(2), "ffn2d": ffn2(3), "qkv": qkv,
                      "scores": head_scores, "pv": head_outputs, "heads": heads_rden, "proj": proj}
            walk(0, opening, stages)
            with pe.Fori(0, PAIRS - 1) as it:
                walk(it, to_a, stages)
                walk(it + 1, to_b, stages)
            walk(PAIRS - 1, closing, stages)


_INS = ["x", "adj", "L0_gnn_w", "L0_gnn_a1", "L0_gnn_a2", "L1_gnn_attn_w", "L1_gnn_attn_b", "L1_gnn_W1",
        "L1_gnn_b1", "L1_gnn_W2", "L1_gnn_b2", "L1_gnn_g1", "L1_gnn_beta1", "L1_gnn_g2", "L1_gnn_beta2",
        "L2_gnn_W", "L2_gnn_a", "L3_gnn_Wq", "L3_gnn_Wk", "L3_gnn_Wv", "L3_gnn_Wo"]


def kernel(**inputs):
    import numpy as np
    import concourse.bacc as bacc
    from concourse.bass_utils import run_bass_kernel_spmd as run

    nc = bacc.Bacc("TRN2", target_bir_lowering=False, num_devices=1)
    arrays, args = {}, []
    for name in _INS:
        a = np.ascontiguousarray(inputs[name])
        arrays[f"in_{name}"] = a
        args.append(nc.dram_tensor(f"in_{name}", a.shape, mybir.dt.from_np(a.dtype), kind="ExternalInput").ap())
    out = nc.dram_tensor("out", arrays["in_x"].shape, F32, kind="ExternalOutput").ap()
    build(nc, *args, out)
    r = run(nc, [arrays], core_ids=[0])
    return r.results[0]["out"]
```

```python
from contextlib import ExitStack

import concourse.bass as bass
from concourse import mybir

F32 = mybir.dt.float32
BF16 = mybir.dt.bfloat16
F32R = mybir.dt.float32r
I32 = mybir.dt.int32
ALU = mybir.AluOpType
ACT = mybir.ActivationFunctionType

P = 128
MASKED = -1e30
LOWEST = -3e38
EPS = 1e-5
TOPK = 16
ALPHA = {"L0": 0.1, "L1.0": 0.2, "L1.1": 0.2, "L1.2": 0.2, "L2": 0.2}
SLOTS = 2


class Batch:

    def __init__(self, it, ahead):
        self.it, self.ahead = it, ahead

    def times(self, count, plus=0):
        return self.it * count + (self.ahead * count + plus)

    def next(self):
        return Batch(self.it, self.ahead + 1)

    def is_number(self, number):
        return isinstance(self.it, int) and self.it + self.ahead == number


class Events:

    def __init__(self, sems, events, first=0):
        self.sems, self.first, self.base, total = sems, first, {}, 0
        for key, count in events:
            self.base[key] = total
            total += count
        self.per_batch = total

    def index(self, key, n=0):
        return self.base[key] + n

    def value(self, it, key, n=0):
        return it.times(self.per_batch, self.first + self.base[key] + n + 1)


def build(nc, x, adj, w0, a01, a02, attn_w, attn_b, w1, b1, w2, b2, g1, beta1, g2, beta2,
          w2g, a2g, wq, wk, wv, wo, out):
    B, N, D = x.shape
    L, _, F = w1.shape
    NT = N // P
    DC = D // P
    FC = F // P
    NH = 8
    DK = D // NH
    HPC = P // DK
    DA = D + 2
    PAIRS = B // SLOTS
    L1K = [f"L1.{l}" for l in range(L)]
    ATT = ["L0"] + L1K + ["L2"]
    HEADS = [f"head{h}" for h in range(NH)]

    A, Bs = 0, 1

    HALF = [
        ("middle", "L0", "v2"), ("ending", "L1.2", "ffn1c ffn2b"), ("middle", "L0", "bc alphaz lrelu"),
        ("ending", "L1.2", "ffn1d"), ("middle", "L0", "exp"), ("ending", "L1.2", "ffn2c ffn2d"),
        ("middle", "L0", "pT1"), ("ending", "L1.2", "xsum"), ("middle", "L0", "pT2"), ("ending", "L1.2", "xnorm"),
        ("ending", "L1", "l1sum"), ("middle", "L0", "agg sum"), ("ending", "L1", "norm"), ("middle", "L0", "norm"),
        ("ending", "L2", "xT"), ("middle", "L1.0", "xT s bc"), ("ending", "L2", "v1"),
        ("middle", "L1.0", "alphaz lrelu"), ("ending", "L2", "v2"), ("middle", "L1.0", "exp"),
        ("ending", "L2", "bc"), ("middle", "L1.0", "pT1"), ("ending", "L2", "topk alphaz"),
        ("middle", "L1.0", "pT2 agg"), ("ending", "L2", "lrelu exp pT1 pT2 agg"),
        ("middle", "L1.0", "sum norm hT ffn1a"), ("ending", "L2", "sum norm"), ("middle", "L1.0", "ffn1b"),
        ("ending", "L3", "xT v1 v2 q k"), ("middle", "L1.0", "ffn2a"), ("ending", "head0", "stack"),
        ("middle", "L1.0", "ffn1c ffn2b"), ("ending", "head0", "scores1"), ("middle", "L1.0", "ffn1d"),
        ("ending", "head1", "stack"), ("ending", "head0", "scores2"), ("middle", "L1.0", "ffn2c"),
        ("ending", "head2", "stack"), ("ending", "head0", "exp"), ("ending", "head1", "scores1"),
        ("middle", "L1.0", "ffn2d xsum"), ("ending", "head1", "scores2"), ("ending", "head0", "pT1"),
        ("ending", "head3", "stack"), ("middle", "L1.0", "xnorm"), ("ending", "head1", "exp"),
        ("ending", "head0", "pT2"), ("middle", "L1.1", "xT"), ("ending", "head2", "scores1"),
        ("middle", "L1.1", "s"), ("ending", "head2", "scores2"), ("middle", "L1.1", "bc"),
        ("ending", "head1", "pT1 pT2 pv"), ("middle", "L1.1", "alphaz lrelu"), ("ending", "head2", "exp"),
        ("ending", "head4", "stack"), ("ending", "head3", "scores1 scores2"), ("middle", "L1.1", "exp pT1"),
        ("ending", "head2", "pT1"), ("ending", "head5", "stack"), ("middle", "L1.1", "pT2"),
        ("ending", "head2", "pT2"), ("middle", "L1.1", "agg"), ("ending", "head3", "exp"),
        ("middle", "L1.1", "sum"), ("ending", "head4", "scores1 scores2"), ("middle", "L1.1", "norm"),
        ("ending", "head3", "pT1 pT2"), ("middle", "L1.1", "hT"), ("ending", "head4", "exp"),
        ("ending", "head3", "pv"), ("ending", "head6", "stack"), ("ending", "head5", "scores1"),
        ("middle", "L1.1", "ffn1a"), ("ending", "head5", "scores2"), ("middle", "L1.1", "ffn1b"),
        ("ending", "head4", "pT1"), ("middle", "L1.1", "ffn2a ffn1c"), ("ending", "head4", "pT2"),
        ("ending", "head5", "exp"), ("middle", "L1.1", "ffn2b"), ("ending", "head7", "stack"),
        ("ending", "head6", "scores1"), ("middle", "L1.1", "ffn1d ffn2c"), ("ending", "head6", "scores2"),
        ("ending", "head5", "pT1 pT2"), ("middle", "L1.1", "ffn2d"), ("ending", "head5", "pv"),
        ("middle", "L1.1", "xsum"), ("ending", "head7", "scores1"), ("middle", "L1.1", "xnorm"),
        ("ending", "head6", "exp"), ("ending", "head7", "scores2"), ("middle", "L1.2", "xT"),
        ("ending", "head6", "pT1"), ("ending", "head7", "exp"), ("middle", "L1.2", "s"),
        ("ending", "head6", "pT2"), ("middle", "L1.2", "bc"), ("ending", "head7", "pT1 pT2"),
        ("middle", "L1.2", "alphaz lrelu exp"), ("ending", "head7", "pv"), ("middle", "L1.2", "pT1"),
        ("ending", "L3", "heads"), ("middle", "L1.2", "pT2 agg sum norm"), ("ending", "L3", "proj"),
        ("middle", "L1.2", "hT"), ("ending", "L3", "ysum norm load store"), ("starting", "L0", "masks xT"),
        ("middle", "L1.2", "ffn1a ffn1b ffn2a"), ("starting", "L0", "v1"),
    ]

    def half_batch(middle, other, after, ending=True, starting=True):
        place = {"middle": (middle, 0), "ending": (other, after), "starting": (other, after + 1)}
        left_out = ([] if ending else ["ending"]) + ([] if starting else ["starting"])
        return [place[part] + (stage, key) for part, key, stages in HALF if part not in left_out
                for stage in stages.split()]

    def only(wanted, slot):
        return [(slot, 0, stage, key) for part, key, stages in HALF if part == wanted for stage in stages.split()]

    A, Bs = 0, 1
    opening = only("starting", A) + half_batch(A, Bs, -1, ending=False)
    to_a = half_batch(Bs, A, 0)
    to_b = half_batch(A, Bs, -1)
    closing = half_batch(Bs, A, 0, starting=False) + only("ending", Bs)

    with ExitStack() as ctx:
        def sb(name, shape, dt=F32):
            return ctx.enter_context(nc.sbuf_tensor(name, shape, dt))

        def pair(name, shape, dt=F32):
            return [sb(f"{name}_{s}", shape, dt) for s in range(SLOTS)]

        def sem(name):
            return ctx.enter_context(nc.semaphore(name))

        def signal(name, events, first=0):
            return Events([sem(f"{name}_{s}") for s in range(SLOTS)], events, first)

        ident = sb("ident", [P, P])
        no_diag = sb("no_diag", [P, P], BF16)
        minus_half = sb("minus_half", [P, NT])
        w0_sb = sb("w0_sb", [P, DC, DA])
        wg_sb = sb("wg_sb", [P, DC, DA])
        aw_sb = sb("aw_sb", [P, L, DC, 2])
        ab_sb = sb("ab_sb", [P, L, NT, 2])
        w1_sb = sb("w1_sb", [P, L, DC, F])
        b1_sb = sb("b1_sb", [P, L, FC])
        w2_sb = sb("w2_sb", [P, L, FC, D])
        g1t_sb = sb("g1t_sb", [P, L, DC])
        beta1t_sb = sb("beta1t_sb", [P, L, DC])
        g2t_sb = sb("g2t_sb", [P, L, DC])
        beta2t_sb = sb("beta2t_sb", [P, L, DC])
        g1_sb = sb("g1_sb", [P, L, D])
        c1_sb = sb("c1_sb", [P, L, D])
        g2_sb = sb("g2_sb", [P, L, D])
        beta2_sb = sb("beta2_sb", [P, L, D])
        wq_sb = sb("wq_sb", [P, DC, D])
        wk_sb = sb("wk_sb", [P, DC, D])
        wv_sb = sb("wv_sb", [P, DC, D])
        wo_sb = sb("wo_sb", [P, DC, D])
        head_rows = sb("head_rows", [NH, DC, P])

        gT = sb("gT", [P, FC // 2, N])
        PT2 = sb("PT2", [P, 2, NT, N])
        q4 = sb("q4", [P, 2, N], F32R)
        k4 = sb("k4", [P, 2, N], F32R)

        HX = pair("HX", [P, NT, D])
        X = pair("X", [P, NT, D])
        X1 = pair("X1", [P, NT, D])
        R = pair("R", [P, NT, D])
        XT = pair("XT", [P, DC, N])
        V = pair("V", [P, NT, DA])
        T = pair("T", [P, NT, N])
        PT = pair("PT", [P, NT, N])
        neg0 = pair("neg0", [P, NT, N], BF16)
        neg1 = pair("neg1", [P, NT, N], BF16)
        s12 = pair("s12", [P, NT, 2])
        row_max = pair("row_max", [P, NT])
        neg_z = pair("neg_z", [P, NT])
        alpha_target = pair("alpha_target", [P, NT])
        neg_max = pair("neg_max", [P, NT])
        den = pair("den", [P, NT])
        rden = pair("rden", [P, NT])
        top = pair("top", [P, NT, TOPK])
        stats = pair("stats", [P, NT, 6])
        mean_var = pair("mean_var", [P, NT, 2])
        var_eps = pair("var_eps", [P, NT])
        rstd = pair("rstd", [P, NT])
        has_edge = pair("has_edge", [P, NT])
        edge_nan = pair("edge_nan", [P, NT])
        den3 = pair("den3", [P, NT, NH])
        rden3 = pair("rden3", [P, NT, NH])

        def flat(bank):
            return bank[:].rearrange("p a b -> p (a b)")

        def chunks(ap):
            return ap.rearrange("p a b -> p (a b)").rearrange("p (c n) -> p c n", c=DC)

        q_hi = [chunks(R[s][:]) for s in range(SLOTS)]
        k_hi = [chunks(X[s][:]) for s in range(SLOTS)]
        q_lo = [chunks(HX[s][:]) for s in range(SLOTS)]
        k_lo = [chunks(neg1[s][:].bitcast(F32)) for s in range(SLOTS)]

        work = [[ctx.enter_context(nc.psum_tensor(f"work_{s}_{i}", [P, N], F32)) for i in range(2)]
                for s in range(SLOTS)]
        acc = [[ctx.enter_context(nc.psum_tensor(f"acc_{s}_{i}", [P, 2, D], F32)) for i in range(NT // 2)]
               for s in range(SLOTS)]

        loaded = sem("loaded")
        consts = sem("consts")
        folded = sem("folded")
        held = {engine: sem(f"held_{engine}") for engine in ("vector", "sync", "gpsimd")}
        x_in = signal("x_in", [("L0", 16)])
        adj_in = signal("adj_in", [("L0", 16)])
        sent = signal("sent", [("L3", 16)], first=16)
        masked = signal("masked", [("L0", 3)])

        uses = []
        for k in ATT:
            uses += [(f"xT {k}", DC), (f"s {k}", 1) if k in L1K else (f"v {k}", NT), (f"bc {k}", 1), (f"pT {k}", NT)]
            if k in L1K:
                uses += [(f"hT {k}", DC), (f"g {k}", FC)]
        uses += [("xT L3", DC), ("v L3", NT), ("q L3", DC), ("k L3", DC)]
        for k, stage in [(0, "scores"), (1, "scores"), (0, "pT")] + [
                q for h in range(2, NH) for q in ((h, "scores"), (h - 1, "pT"))] + [(NH - 1, "pT")]:
            uses.append((f"{stage} {HEADS[k]}", NT))
        uses += [("rdenT L3", 2), ("rden L3", DC)]
        turn = Events(None, uses)
        assert turn.per_batch % 2 == 0
        per_bank = turn.per_batch // 2
        filled = [[sem(f"filled_{s}_{i}") for i in range(2)] for s in range(SLOTS)]
        evacuated = [[sem(f"evacuated_{s}_{i}") for i in range(2)] for s in range(SLOTS)]

        acc_uses = [("L0", 1)] + [(k + c, 1) for k in L1K for c in ("", " ffn")] + [("L2", 1), ("heads", 1), ("L3", 1)]
        acc_filled = signal("acc_filled", [(k, 1 if k == "heads" else NT // 2) for k, _ in acc_uses])
        acc_evacuated = signal("acc_evacuated", acc_uses, first=1)

        neg_z_ready = signal("neg_z_ready", [(k, 1) for k in ATT])
        neg_max_ready = signal("neg_max_ready", [(k, 1) for k in ATT + HEADS])
        edge_step = signal("edge_step", [("L0", 3)])
        topk_step = signal("topk_step", [("L2", 3 * NT)])
        alpha_target_ready = signal("alpha_target_ready", [(k, 1) for k in ATT])
        alpha_z_done = signal("alpha_z_done", [(k, NT) for k in ATT])
        lrelu_done = signal("lrelu_done", [(k, NT) for k in ATT])
        exp_done = signal("exp_done", [(k, NT) for k in ATT + HEADS])
        split = signal("split", [("q", DC), ("k", DC)])
        stacked = [signal(f"stacked{i}", [(k, 8 * 16) for k in HEADS[i::2]]) for i in range(2)]
        kept = signal("kept", [("L2", NT)])
        rden_ready = signal("rden_ready", [(k, 1) for k in ATT + ["L3"]])
        elu_step = signal("elu_step", [("L0", 2), ("L2", 2)])
        sum_ready = signal("sum_ready", [(k, 1) for k in ("L0", "L1", "L2")])
        norms = [(k, 1) for k in ["L0"] + [q + c for q in L1K for c in (" h", " x")] + ["L1", "L2", "L3"]]
        stats_ready = signal("stats_ready", norms)
        mean_ready = signal("mean_ready", norms)
        var_ready = signal("var_ready", norms)
        rstd_ready = signal("rstd_ready", norms)
        normed = signal("normed", norms)
        affines = [(k + c, 1) for k in L1K for c in (" h", " x")][:-1]
        affine_half = signal("affine_half", affines)
        affine_done = signal("affine_done", affines)
        x1_shifted = signal("x1_shifted", [("L1", 1)])
        scaled = signal("scaled", [("L1", 1)])

        def hold(eng, name="vector"):
            eng.sem_inc(held[name], 1)

        class Use:

            def __init__(self, s, it, key, n=0):
                i = turn.index(key, n)
                self.bank = work[s][i % 2]
                self.filled, self.evacuated = filled[s][i % 2], evacuated[s][i % 2]
                self.turn = it.times(per_bank, i // 2 + 1)

        def target_score(s, key, t):
            return s12[s][:, t, 0:1] if key in L1K else V[s][:, t, D:D + 1]

        def tiles(half):
            return range(half * NT // 2, (half + 1) * NT // 2)

        def weights(s, key):
            return PT[s] if key in HEADS and HEADS.index(key) % 2 else T[s]

        def transposed(s, key):
            return PT2[:, HEADS.index(key) % 2] if key in HEADS else PT[s]

        SOURCE = {"L0": HX, "L1.0": X1, "L1.1": X, "L1.2": X, "L2": X1, "L3": X1}

        def wait_source(eng, s, it, key):
            if key == "L0":
                eng.wait_ge(x_in.sems[s], x_in.value(it, "L0", 15))
            elif key in ("L1.1", "L1.2"):
                eng.wait_ge(affine_done.sems[s], affine_done.value(it, L1K[L1K.index(key) - 1] + " x"))
            else:
                eng.wait_ge(normed.sems[s], normed.value(it, {"L1.0": "L0", "L2": "L1", "L3": "L2"}[key]))

        def walk(it, order, stages):
            for s, ahead, stage, key in order:
                if stage in stages:
                    stages[stage](s, Batch(it, ahead), key)

        N_LOADS = 6 + L * (2 * DC + 7 + 5) + 4
        N_CONSTS = 8
        N_FOLDED = 4 * DC + 2 * L + 1

        block = ctx.enter_context(nc.Block())

        @block.sync
        def _(sp):
            n_loads = [0]

            def load(dst, src):
                sp.dma_start(dst, src).then_inc(loaded, 16)
                n_loads[0] += 1

            def load_columns(dst, src):
                sp.dma_start(dst, src.rearrange("(c p) -> p c", p=P), allow_slow_non_contiguous=True)\
                    .then_inc(loaded, 16)
                n_loads[0] += 1

            def load_x(s, it):
                sp.dma_start(HX[s][:], x[it.times(SLOTS, s)].rearrange("(t p) d -> p t d", p=P)).then_inc(x_in.sems[s], 16)

            def row(src):
                return src.rearrange("(o d) one -> o (d one)", o=1)

            for s in range(SLOTS):
                sp.sem_inc(sent.sems[s], 16)
            load_x(0, Batch(0, 0))
            load_x(1, Batch(0, 0))
            load(w0_sb[:, :, 0:D], w0.rearrange("(c p) n -> p c n", p=P))
            load(PT2[:, 0, 0, 0:D], row(a01).broadcast_to([P, D]))
            load(PT2[:, 0, 1, 0:D], row(a02).broadcast_to([P, D]))
            load(PT2[:, 0, 2, 0:2 * D], row(a2g).broadcast_to([P, 2 * D]))
            load(PT2[:, 0, 3, 0:L], attn_b.rearrange("(o l) -> o l", o=1).broadcast_to([P, L]))
            load(wg_sb[:, :, 0:D], w2g.rearrange("(c p) n -> p c n", p=P))
            for l in range(L):
                for half in range(2):
                    for c in range(DC):
                        load(aw_sb[:, l, c, half:half + 1],
                             attn_w[l, half * D + c * P:half * D + (c + 1) * P].rearrange("(p one) -> p one", one=1))
                load(w1_sb[:, l], w1[l].rearrange("(c p) f -> p c f", p=P))
                load(w2_sb[:, l], w2[l].rearrange("(c p) n -> p c n", p=P))
                load_columns(b1_sb[:, l], b1[l])
                load_columns(g1t_sb[:, l], g1[l])
                load_columns(beta1t_sb[:, l], beta1[l])
                load_columns(g2t_sb[:, l], g2[l])
                load_columns(beta2t_sb[:, l], beta2[l])
                for dst, src in ((g1_sb[:, l], g1), (c1_sb[:, l], beta1), (PT2[:, 1, l, 0:D], b2),
                                 (g2_sb[:, l], g2), (beta2_sb[:, l], beta2)):
                    load(dst, src[l:l + 1, :].broadcast_to([P, D]))
            for dst, src in ((wq_sb, wq), (wk_sb, wk), (wv_sb, wv), (wo_sb, wo)):
                load(dst[:], src.rearrange("(c p) n -> p c n", p=P))
            assert n_loads[0] == N_LOADS

            def load_next(s, it, key):
                if it.is_number(PAIRS - 1):
                    return
                sp.wait_ge(stacked[1].sems[s], stacked[1].value(it, HEADS[-1], 8 * 16 - 1))
                hold(sp, "sync")
                load_x(s, it.next())

            def stack(s, it, key):
                h = HEADS.index(key)
                m, r = h // HPC, h % HPC * DK
                if h == 0:
                    u = Use(s, it, "k L3", 0)
                    sp.wait_ge(u.evacuated, u.turn + 1)
                    hold(sp, "sync")
                    u = Use(s, it, "k L3", 1)
                    sp.wait_ge(u.evacuated, u.turn + 1)
                    hold(sp, "sync")
                elif h > 1:
                    u = Use(s, it, f"scores {HEADS[h - 2]}", NT - 1)
                    sp.wait_ge(u.filled, u.turn)
                    hold(sp, "sync")
                for row, (q_half, k_half) in enumerate(((q_hi, k_hi), (q_hi, k_lo), (q_lo, k_hi), (q_lo, k_lo))):
                    for dst, src in ((q4, q_half), (k4, k_half)):
                        sp.dma_start(dst[row * DK:(row + 1) * DK, h % 2, :].bitcast(F32), src[s][r:r + DK, m, :])\
                            .then_inc(stacked[h % 2].sems[s], 16)

            def store(s, it, key):
                sp.wait_ge(normed.sems[s], normed.value(it, "L3"))
                hold(sp, "sync")
                sp.dma_start(out[it.times(SLOTS, s)].rearrange("(t p) d -> p t d", p=P), X[s][:]).then_inc(sent.sems[s], 16)

            stages = {"load": load_next, "stack": stack, "store": store}
            walk(0, opening, stages)
            with sp.Fori(0, PAIRS - 1) as it:
                walk(it, to_a, stages)
                walk(it + 1, to_b, stages)
            walk(PAIRS - 1, closing, stages)
            for s in range(SLOTS):
                sp.wait_ge(sent.sems[s], sent.value(Batch(PAIRS - 1, 0), "L3", 15))

        @block.gpsimd
        def _(pool):
            def load_adj(s, it):
                pool.dma_start(neg1[s][:], adj[it.times(SLOTS, s)].rearrange("(t p) j -> p t j", p=P))\
                    .then_inc(adj_in.sems[s], 16)

            for s in range(SLOTS):
                load_adj(s, Batch(0, 0))
            pool.memset(ident[:], 0.0).then_inc(consts, 1)
            pool.memset(no_diag[:], 1.0).then_inc(consts, 1)
            pool.memset(minus_half[:], -0.5).then_inc(consts, 1)
            pool.memset(head_rows[:], 1.0).then_inc(consts, 1)
            pool.wait_ge(consts, 4)
            for m, fill_with in ((ident, 1.0), (no_diag, 0.0)):
                pool.affine_select(out=m[:], in_=m[:], compare_op=ALU.not_equal, fill=fill_with, base=0,
                                   pattern=[[-1, P]], channel_multiplier=1).then_inc(consts, 1)
            features = [[P, DC], [1, P]]
            pool.affine_select(out=head_rows[:], in_=head_rows[:], compare_op=ALU.is_ge, fill=0.0, base=0,
                               pattern=features, channel_multiplier=-DK).then_inc(consts, 1)
            pool.wait_ge(consts, N_CONSTS - 1)
            pool.affine_select(out=head_rows[:], in_=head_rows[:], compare_op=ALU.is_ge, fill=0.0, base=DK - 1,
                               pattern=[[-P, DC], [-1, P]], channel_multiplier=DK).then_inc(consts, 1)
            pool.wait_ge(consts, N_CONSTS)
            pool.wait_ge(folded, N_FOLDED)

            def rsqrt(s, it, key):
                pool.wait_ge(var_ready.sems[s], var_ready.value(it, key))
                pool.tensor_tensor(rstd[s][:], var_eps[s][:], minus_half[:], ALU.pow).then_inc(rstd_ready.sems[s], 1)

            def affine(s, it, key, dst, src, gain, shift):
                l = L1K.index(key[:4])
                pool.wait_ge(normed.sems[s], normed.value(it, key))
                pool.tensor_tensor(dst[:], src[:], gain[:, l:l + 1, :].broadcast_to([P, NT, D]), ALU.mult)\
                    .then_inc(affine_half.sems[s], 1)
                pool.wait_ge(affine_half.sems[s], affine_half.value(it, key))
                pool.tensor_tensor(dst[:], dst[:], shift[:, l:l + 1, :].broadcast_to([P, NT, D]), ALU.add)\
                    .then_inc(affine_done.sems[s], 1)

            def after_sum(s, it, key):
                rsqrt(s, it, key + " h" if key in L1K else key)

            def h_affine(s, it, key):
                if key in L1K:
                    affine(s, it, key + " h", R[s], HX[s], g1_sb, c1_sb)

            def after_xsum(s, it, key):
                rsqrt(s, it, key + " x")

            def x_affine(s, it, key):
                if key == L1K[-1]:
                    return
                if key == L1K[0]:
                    pool.wait_ge(sent.sems[s], it.times(16, 16))
                    hold(pool, "gpsimd")
                affine(s, it, key + " x", X[s], HX[s], g2_sb, beta2_sb)
                if key == L1K[0]:
                    pool.tensor_tensor(X1[s][:], X1[s][:], beta2_sb[:, L - 1:L, :].broadcast_to([P, NT, D]), ALU.add)\
                        .then_inc(x1_shifted.sems[s], 1)

            def after_l1sum(s, it, key):
                rsqrt(s, it, "L1")

            def load_next(s, it, key):
                if it.is_number(PAIRS - 1):
                    return
                pool.wait_ge(stacked[1].sems[s], stacked[1].value(it, HEADS[-1], 8 * 16 - 1))
                hold(pool, "gpsimd")
                load_adj(s, it.next())

            stages = {"load": load_next, "sum": after_sum, "norm": h_affine, "xsum": after_xsum, "xnorm": x_affine,
                      "l1sum": after_l1sum, "ysum": rsqrt}
            walk(0, opening, stages)
            with pool.Fori(0, PAIRS - 1) as it:
                walk(it, to_a, stages)
                walk(it + 1, to_b, stages)
            walk(PAIRS - 1, closing, stages)

        @block.vector
        def _(dve):
            dve.wait_ge(loaded, 16 * N_LOADS)
            for c in range(DC):
                for half in range(2):
                    dve.tensor_tensor_reduce(X1[half][:, c, :], w0_sb[:, c, 0:D], PT2[:, 0, half, 0:D], 1.0, 0.0,
                                             ALU.mult, ALU.add, w0_sb[:, c, D + half:D + half + 1]).then_inc(folded, 1)
                    dve.tensor_tensor_reduce(X1[half][:, DC + c, :], wg_sb[:, c, 0:D], PT2[:, 0, 2, half * D:(half + 1) * D],
                                             1.0, 0.0, ALU.mult, ALU.add,
                                             wg_sb[:, c, D + half:D + half + 1]).then_inc(folded, 1)
            for l in range(L):
                dve.tensor_tensor(c1_sb[:, l], c1_sb[:, l], PT2[:, 1, l, 0:D], ALU.add).then_inc(folded, 1)
            dve.memset(ab_sb[:], 0.0).then_inc(folded, 1)
            dve.wait_ge(folded, 4 * DC + L + 1)
            for l in range(L):
                dve.tensor_copy(ab_sb[:, l, :, 0], PT2[:, 0, 3, l:l + 1].broadcast_to([P, NT])).then_inc(folded, 1)
            dve.wait_ge(folded, N_FOLDED)
            dve.wait_ge(consts, N_CONSTS)
            for s in range(SLOTS):
                dve.memset(den[s][:], 0.0).then_inc(evacuated[s][0], 1)
                dve.memset(rden[s][:], 0.0).then_inc(evacuated[s][1], 1)
                dve.memset(neg_z[s][:], 0.0).then_inc(acc_evacuated.sems[s], 1)

            def make_masks(s, it, key):
                dve.wait_ge(adj_in.sems[s], adj_in.value(it, "L0", 15))
                dve.tensor_scalar(neg0[s][:], neg1[s][:], 0.0, MASKED, ALU.is_equal, ALU.mult).then_inc(masked.sems[s], 1)
                dve.wait_ge(masked.sems[s], masked.value(it, "L0", 0))
                dve.tensor_copy(neg1[s][:], neg0[s][:]).then_inc(masked.sems[s], 1)
                dve.wait_ge(masked.sems[s], masked.value(it, "L0", 1))
                for t in range(NT):
                    last = dve.tensor_tensor(neg1[s][:, t, t * P:(t + 1) * P], neg0[s][:, t, t * P:(t + 1) * P],
                                             no_diag[:], ALU.mult)
                last.then_inc(masked.sems[s], 1)
                dve.wait_ge(masked.sems[s], masked.value(it, "L0", 2))

            def x_transposed(s, it, key):
                u = Use(s, it, f"xT {key}", 1)
                dve.wait_ge(u.filled, u.turn)
                if key in L1K[1:]:
                    l = L1K.index(key) - 1
                    dve.tensor_scalar(XT[s][:, 1, :], u.bank[:], g2t_sb[:, l, 1:2], beta2t_sb[:, l, 1:2], ALU.mult, ALU.add)\
                        .then_inc(u.evacuated, 1)
                else:
                    dve.tensor_copy(XT[s][:, 1, :], u.bank[:]).then_inc(u.evacuated, 1)

            def scores_of_x(s, it, key):
                u = Use(s, it, f"s {key}")
                dve.wait_ge(u.filled, u.turn)
                dve.tensor_tensor(s12[s][:], u.bank[:, 0:NT * 2].rearrange("p (t k) -> p t k", k=2),
                                  ab_sb[:, L1K.index(key)], ALU.add).then_inc(u.evacuated, 1)

            def masked_max(s, it, key):
                u = Use(s, it, f"bc {key}")
                dve.wait_ge(u.filled, u.turn)
                neg = neg1 if key in L1K else neg0
                hold(dve)
                for t in range(NT):
                    last = dve.tensor_tensor_reduce(T[s][:, t, :], u.bank[:], neg[s][:, t, :], 1.0, LOWEST,
                                                    ALU.add, ALU.max, row_max[s][:, t:t + 1])
                last.then_inc(u.evacuated, 1)
                u = Use(s, it, f"bc {key}")
                dve.wait_ge(u.evacuated, u.turn + 1)
                target = s12[s][:, :, 0] if key in L1K else V[s][:, :, D]
                dve.scalar_tensor_tensor(neg_z[s][:], row_max[s][:], -1.0, target, ALU.mult, ALU.subtract)\
                    .then_inc(neg_z_ready.sems[s], 1)
                if key == "L0":
                    dve.tensor_scalar(has_edge[s][:], row_max[s][:], 0.5 * MASKED, None, ALU.is_gt)\
                        .then_inc(edge_step.sems[s], 1)
                    dve.wait_ge(edge_step.sems[s], edge_step.value(it, "L0", 0))
                    dve.reciprocal(edge_nan[s][:], has_edge[s][:]).then_inc(edge_step.sems[s], 1)
                    dve.wait_ge(edge_step.sems[s], edge_step.value(it, "L0", 1))
                    dve.tensor_tensor(edge_nan[s][:], edge_nan[s][:], has_edge[s][:], ALU.mult)\
                        .then_inc(edge_step.sems[s], 1)
                dve.tensor_scalar(alpha_target[s][:], target, ALPHA[key], None, ALU.mult)\
                    .then_inc(alpha_target_ready.sems[s], 1)
                dve.wait_ge(neg_z_ready.sems[s], neg_z_ready.value(it, key))
                dve.scalar_tensor_tensor(neg_max[s][:], neg_z[s][:], ALPHA[key], neg_z[s][:], ALU.mult, ALU.min)\
                    .then_inc(neg_max_ready.sems[s], 1)

            def topk(s, it, key):
                for t in range(NT):
                    dve.max(top[s][:, t, 0:8], T[s][:, t, :]).then_inc(topk_step.sems[s], 1)
                for t in range(NT):
                    dve.wait_ge(topk_step.sems[s], topk_step.value(it, "L2", t))
                    hold(dve)
                    dve.match_replace(PT[s][:, t, :], top[s][:, t, 0:8], T[s][:, t, :], LOWEST)\
                        .then_inc(topk_step.sems[s], 1)
                for t in range(NT):
                    dve.wait_ge(topk_step.sems[s], topk_step.value(it, "L2", NT + t))
                    hold(dve)
                    dve.max(top[s][:, t, 8:16], PT[s][:, t, :]).then_inc(topk_step.sems[s], 1)

            def lrelu(s, it, key):
                dst = PT[s] if key == "L2" else T[s]
                for t in range(NT):
                    dve.wait_ge(alpha_z_done.sems[s], alpha_z_done.value(it, key, t))
                    dve.scalar_tensor_tensor(dst[:, t, :], T[s][:, t, :], target_score(s, key, t), PT[s][:, t, :],
                                             ALU.add, ALU.max).then_inc(lrelu_done.sems[s], 1)

            def weights_transposed(half):
                def stage(s, it, key):
                    if key == "L2" and half == 0:
                        dve.wait_ge(topk_step.sems[s], topk_step.value(it, "L2", 3 * NT - 1))
                        for t in range(NT):
                            dve.wait_ge(exp_done.sems[s], exp_done.value(it, key, t))
                            dve.scalar_tensor_tensor(T[s][:, t, :], T[s][:, t, :], top[s][:, t, TOPK - 1:TOPK],
                                                     PT[s][:, t, :], ALU.is_ge, ALU.mult).then_inc(kept.sems[s], 1)
                    if key in ATT and half == 1:
                        dve.wait_ge(exp_done.sems[s], exp_done.value(it, key, NT - 1))
                        dve.reciprocal(rden[s][:], den[s][:]).then_inc(rden_ready.sems[s], 1)
                    if key in ATT:
                        dve.wait_ge(lrelu_done.sems[s], lrelu_done.value(it, key, NT - 1))
                    dst = transposed(s, key)
                    for t in tiles(half)[1::2]:
                        u = Use(s, it, f"pT {key}", t)
                        dve.wait_ge(u.filled, u.turn)
                        dve.tensor_copy(dst[:, :, t * P:(t + 1) * P], u.bank[:].rearrange("p (j n) -> p j n", j=NT))\
                            .then_inc(u.evacuated, 1)
                return stage

            def statistics(s, it, key):
                for t in range(NT):
                    last = dve.bn_stats(stats[s][:, t, :], R[s][:, t, :])
                last.then_inc(stats_ready.sems[s], 1)
                dve.wait_ge(stats_ready.sems[s], stats_ready.value(it, key))
                hold(dve)
                for t in range(NT):
                    last = dve.bn_aggr(mean_var[s][:, t, :], stats[s][:, t, :])
                last.then_inc(mean_ready.sems[s], 1)
                dve.wait_ge(mean_ready.sems[s], mean_ready.value(it, key))
                dve.tensor_scalar(var_eps[s][:], mean_var[s][:, :, 1], EPS, None, ALU.add).then_inc(var_ready.sems[s], 1)

            def normalize(s, it, key, dst):
                dve.wait_ge(rstd_ready.sems[s], rstd_ready.value(it, key))
                for t in range(NT):
                    last = dve.tensor_scalar(dst[:, t, :], R[s][:, t, :], mean_var[s][:, t, 0:1], rstd[s][:, t:t + 1],
                                             ALU.subtract, ALU.mult)
                last.then_inc(normed.sems[s], 1)

            def aggregated(s, it, key):
                if key in L1K:
                    wait_source(dve, s, it, key)
                    dve.wait_ge(rden_ready.sems[s], rden_ready.value(it, key))
                    for t in range(NT):
                        if t % 2 == 0:
                            dve.wait_ge(acc_filled.sems[s], acc_filled.value(it, key, t // 2))
                        last = dve.scalar_tensor_tensor(R[s][:, t, :], acc[s][t // 2][:, t % 2, :], rden[s][:, t:t + 1],
                                                        SOURCE[key][s][:, t, :], ALU.mult, ALU.add)
                    last.then_inc(acc_evacuated.sems[s], 1)
                    dve.wait_ge(acc_evacuated.sems[s], acc_evacuated.value(it, key))
                    statistics(s, it, key + " h")
                else:
                    E = T[s][:, :, 0:D]
                    dve.wait_ge(acc_evacuated.sems[s], acc_evacuated.value(it, key))
                    dve.tensor_scalar(E, E, 1.0, -1.0, ALU.min, ALU.add).then_inc(elu_step.sems[s], 1)
                    dve.wait_ge(elu_step.sems[s], elu_step.value(it, key, 0))
                    dve.tensor_tensor(R[s][:], R[s][:], E, ALU.max).then_inc(elu_step.sems[s], 1)
                    dve.wait_ge(elu_step.sems[s], elu_step.value(it, key, 1))
                    dve.tensor_tensor(R[s][:], R[s][:], SOURCE[key][s][:], ALU.add).then_inc(sum_ready.sems[s], 1)
                    dve.wait_ge(sum_ready.sems[s], sum_ready.value(it, key))
                    statistics(s, it, key)

            def norm(s, it, key):
                if key in L1K:
                    normalize(s, it, key + " h", HX[s])
                elif key == "L3":
                    normalize(s, it, key, X[s])
                else:
                    normalize(s, it, key, X1[s])

            def h_transposed(s, it, key):
                l = L1K.index(key)
                u = Use(s, it, f"hT {key}", 1)
                dve.wait_ge(u.filled, u.turn)
                dve.tensor_scalar(XT[s][:, 1, :], u.bank[:], g1t_sb[:, l, 1:2], beta1t_sb[:, l, 1:2], ALU.mult, ALU.add)\
                    .then_inc(u.evacuated, 1)

            def after_ffn(s, it, key):
                dve.wait_ge(affine_done.sems[s], affine_done.value(it, key + " h"))
                for i in range(NT // 2):
                    dve.wait_ge(acc_filled.sems[s], acc_filled.value(it, key + " ffn", i))
                    last = dve.tensor_tensor(R[s][:, 2 * i:2 * i + 2, :], acc[s][i][:], R[s][:, 2 * i:2 * i + 2, :],
                                             ALU.add)
                last.then_inc(acc_evacuated.sems[s], 1)
                dve.wait_ge(acc_evacuated.sems[s], acc_evacuated.value(it, key + " ffn"))
                statistics(s, it, key + " x")

            def x_norm(s, it, key):
                normalize(s, it, key + " x", HX[s])

            def l1_sum(s, it, key):
                dve.wait_ge(normed.sems[s], normed.value(it, L1K[-1] + " x"))
                dve.tensor_tensor(R[s][:], HX[s][:], g2_sb[:, L - 1:L, :].broadcast_to([P, NT, D]), ALU.mult)\
                    .then_inc(scaled.sems[s], 1)
                dve.wait_ge(x1_shifted.sems[s], x1_shifted.value(it, "L1"))
                dve.wait_ge(scaled.sems[s], scaled.value(it, "L1"))
                dve.tensor_tensor(R[s][:], R[s][:], X1[s][:], ALU.add).then_inc(sum_ready.sems[s], 1)
                dve.wait_ge(sum_ready.sems[s], sum_ready.value(it, "L1"))
                statistics(s, it, "L1")

            def lower_halves(name, hi, lo, scale):
                def stage(s, it, key):
                    for c in range(DC):
                        u = Use(s, it, f"{name} L3", c)
                        dve.wait_ge(split.sems[s], split.value(it, name, c))
                        dve.scalar_tensor_tensor(lo[s][:, c, :].bitcast(F32R), u.bank[:], scale, hi[s][:, c, :],
                                                 ALU.mult, ALU.subtract).then_inc(u.evacuated, 1)
                return stage

            def head_scores(half):
                def stage(s, it, key):
                    dst = weights(s, key)
                    h = HEADS.index(key)
                    if h and half == 0:
                        dve.wait_ge(neg_max_ready.sems[s], neg_max_ready.value(it, HEADS[h - 1]))
                    for t in tiles(half):
                        u = Use(s, it, f"scores {key}", t)
                        dve.wait_ge(u.filled, u.turn)
                        hold(dve)
                        dve.tensor_tensor_reduce(dst[:, t, :], u.bank[:], neg0[s][:, t, :], 1.0, LOWEST, ALU.add, ALU.max,
                                                 row_max[s][:, t:t + 1]).then_inc(u.evacuated, 1)
                    if half == 0:
                        return
                    if h:
                        dve.wait_ge(exp_done.sems[s], exp_done.value(it, HEADS[h - 1], NT - 1))
                    u = Use(s, it, f"scores {key}", NT - 2)
                    dve.wait_ge(u.evacuated, u.turn + 1)
                    u = Use(s, it, f"scores {key}", NT - 1)
                    dve.wait_ge(u.evacuated, u.turn + 1)
                    dve.tensor_scalar(neg_max[s][:], row_max[s][:], -1.0, None, ALU.mult).then_inc(neg_max_ready.sems[s], 1)
                return stage

            def heads_normed(s, it, key):
                dve.wait_ge(exp_done.sems[s], exp_done.value(it, HEADS[-1], NT - 1))
                dve.reciprocal(rden3[s][:], den3[s][:]).then_inc(rden_ready.sems[s], 1)
                dve.wait_ge(acc_filled.sems[s], acc_filled.value(it, "heads"))
                for m in range(DC):
                    u = Use(s, it, "rden L3", m)
                    dve.wait_ge(u.evacuated, u.turn + 1)
                    last = dve.scalar_tensor_tensor(XT[s][:, m, :], flat(acc[s][m]), 0.0, chunks(R[s][:])[:, m, :],
                                                    ALU.max, ALU.mult)
                last.then_inc(acc_evacuated.sems[s], 1)

            def after_proj(s, it, key):
                for t in range(NT):
                    if t % 2 == 0:
                        dve.wait_ge(acc_filled.sems[s], acc_filled.value(it, "L3", t // 2))
                    last = dve.scalar_tensor_tensor(R[s][:, t, :], X1[s][:, t, :], edge_nan[s][:, t:t + 1],
                                                    acc[s][t // 2][:, t % 2, :], ALU.mult, ALU.add)
                last.then_inc(acc_evacuated.sems[s], 1)
                dve.wait_ge(acc_evacuated.sems[s], acc_evacuated.value(it, "L3"))
                statistics(s, it, "L3")

            stages = {"masks": make_masks, "xT": x_transposed, "s": scores_of_x, "bc": masked_max, "topk": topk,
                      "lrelu": lrelu, "pT1": weights_transposed(0), "pT2": weights_transposed(1), "sum": aggregated, "norm": norm, "hT": h_transposed,
                      "xsum": after_ffn, "xnorm": x_norm, "l1sum": l1_sum, "q": lower_halves("q", q_hi, q_lo, float(DK) ** -0.5), "k": lower_halves("k", k_hi, k_lo, 1.0),
                      "scores1": head_scores(0), "scores2": head_scores(1),
                      "heads": heads_normed, "ysum": after_proj}
            walk(0, opening, stages)
            with dve.Fori(0, PAIRS - 1) as it:
                walk(it, to_a, stages)
                walk(it + 1, to_b, stages)
            walk(PAIRS - 1, closing, stages)

        @block.scalar
        def _(act):
            act.wait_ge(loaded, 16 * N_LOADS)
            act.wait_ge(folded, N_FOLDED)

            def x_transposed(s, it, key):
                u = Use(s, it, f"xT {key}", 0)
                act.wait_ge(u.filled, u.turn)
                if key in L1K[1:]:
                    l = L1K.index(key) - 1
                    act.activation(XT[s][:, 0, :], u.bank[:], ACT.Identity, scale=g2t_sb[:, l, 0:1],
                                   bias=beta2t_sb[:, l, 0:1]).then_inc(u.evacuated, 1)
                else:
                    act.activation(XT[s][:, 0, :], u.bank[:], ACT.Copy).then_inc(u.evacuated, 1)

            def projected(half):
                def stage(s, it, key):
                    for t in tiles(half):
                        u = Use(s, it, f"v {key}", t)
                        act.wait_ge(u.filled, u.turn)
                        w = D if key == "L3" else DA
                        act.activation(V[s][:, t, 0:w], u.bank[:, 0:w], ACT.Copy).then_inc(u.evacuated, 1)
                return stage

            def alpha_z(s, it, key):
                if key == "L2":
                    act.wait_ge(topk_step.sems[s], topk_step.value(it, "L2", 3 * NT - 1))
                act.wait_ge(alpha_target_ready.sems[s], alpha_target_ready.value(it, key))
                for t in range(NT):
                    act.activation(PT[s][:, t, :], T[s][:, t, :], ACT.Identity, bias=alpha_target[s][:, t:t + 1],
                                   scale=ALPHA[key]).then_inc(alpha_z_done.sems[s], 1)

            def exp(s, it, key):
                if key in HEADS:
                    act.wait_ge(neg_max_ready.sems[s], neg_max_ready.value(it, key))
                    h = HEADS.index(key)
                    z = weights(s, key)
                    for t in range(NT):
                        act.activation(z[:, t, :], z[:, t, :], ACT.Exp, bias=neg_max[s][:, t:t + 1],
                                       accum_out=den3[s][:, t, h:h + 1]).then_inc(exp_done.sems[s], 1)
                    return
                z = PT[s] if key == "L2" else T[s]
                for t in range(NT):
                    act.wait_ge(lrelu_done.sems[s], lrelu_done.value(it, key, t))
                    act.activation(z[:, t, :], z[:, t, :], ACT.Exp, bias=neg_max[s][:, t:t + 1],
                                   accum_out=den[s][:, t:t + 1]).then_inc(exp_done.sems[s], 1)

            def weights_transposed(half):
                def stage(s, it, key):
                    dst = transposed(s, key)
                    for t in tiles(half)[0::2]:
                        u = Use(s, it, f"pT {key}", t)
                        act.wait_ge(u.filled, u.turn)
                        act.activation(dst[:, :, t * P:(t + 1) * P], u.bank[:].rearrange("p (j n) -> p j n", j=NT), ACT.Copy)\
                            .then_inc(u.evacuated, 1)
                return stage

            def agg(s, it, key):
                if key in L1K:
                    return
                act.wait_ge(rden_ready.sems[s], rden_ready.value(it, key))
                for t in range(NT):
                    if t % 2 == 0:
                        act.wait_ge(acc_filled.sems[s], acc_filled.value(it, key, t // 2))
                    act.activation(R[s][:, t, :], acc[s][t // 2][:, t % 2, :], ACT.Copy, scale=rden[s][:, t:t + 1])
                for t in range(NT):
                    last = act.activation(T[s][:, t, 0:D], acc[s][t // 2][:, t % 2, :], ACT.Exp,
                                          scale=rden[s][:, t:t + 1])
                last.then_inc(acc_evacuated.sems[s], 1)

            def h_transposed(s, it, key):
                l = L1K.index(key)
                u = Use(s, it, f"hT {key}", 0)
                act.wait_ge(u.filled, u.turn)
                act.activation(XT[s][:, 0, :], u.bank[:], ACT.Identity, scale=g1t_sb[:, l, 0:1],
                               bias=beta1t_sb[:, l, 0:1]).then_inc(u.evacuated, 1)

            def gelu(quarter):
                def stage(s, it, key):
                    l = L1K.index(key)
                    for f in range(quarter * FC // 4, (quarter + 1) * FC // 4):
                        u = Use(s, it, f"g {key}", f)
                        act.wait_ge(u.filled, u.turn)
                        act.activation(gT[:, f % (FC // 2), :], u.bank[:], ACT.Gelu, bias=b1_sb[:, l, f:f + 1]).then_inc(u.evacuated, 1)
                return stage

            def upper_halves(name, hi, scale):
                def stage(s, it, key):
                    for c in range(DC):
                        u = Use(s, it, f"{name} L3", c)
                        act.wait_ge(u.filled, u.turn)
                        act.activation(hi[s][:, c, :].bitcast(F32R), u.bank[:], ACT.Copy, scale=scale)\
                            .then_inc(split.sems[s], 1)
                return stage

            def heads_rden(s, it, key):
                for i in range(2):
                    u = Use(s, it, "rdenT L3", i)
                    act.wait_ge(u.filled, u.turn)
                    act.activation(T[s][0:NH, 0, i * N // 2:(i + 1) * N // 2], u.bank[0:NH, 0:N // 2], ACT.Copy)\
                        .then_inc(u.evacuated, 1)
                for m in range(DC):
                    u = Use(s, it, "rden L3", m)
                    act.wait_ge(u.filled, u.turn)
                    act.activation(chunks(R[s][:])[:, m, :], u.bank[:], ACT.Copy).then_inc(u.evacuated, 1)

            stages = {"xT": x_transposed, "v1": projected(0), "v2": projected(1), "alphaz": alpha_z, "exp": exp, "pT1": weights_transposed(0),
                      "pT2": weights_transposed(1),
                      "agg": agg, "hT": h_transposed, "ffn1a": gelu(0), "ffn1b": gelu(1), "ffn1c": gelu(2), "ffn1d": gelu(3),
                      "q": upper_halves("q", q_hi, float(DK) ** -0.5), "k": upper_halves("k", k_hi, 1.0), "heads": heads_rden}
            walk(0, opening, stages)
            with act.Fori(0, PAIRS - 1) as it:
                walk(it, to_a, stages)
                walk(it + 1, to_b, stages)
            walk(PAIRS - 1, closing, stages)

        @block.tensor
        def _(pe):
            pe.wait_ge(loaded, 16 * N_LOADS)
            pe.wait_ge(consts, N_CONSTS)
            pe.wait_ge(folded, N_FOLDED)

            def transpose_tiles(s, it, key, n, src, c):
                u = Use(s, it, key, n)
                pe.wait_ge(u.evacuated, u.turn)
                for t in range(NT):
                    last = pe.transpose(u.bank[:, t * P:(t + 1) * P], src[:, t, c * P:(c + 1) * P], ident[:])
                last.then_inc(u.filled, 1)

            def xT(s, it, key):
                if key in L1K[1:]:
                    pe.wait_ge(normed.sems[s], normed.value(it, L1K[L1K.index(key) - 1] + " x"))
                    src = HX[s]
                else:
                    wait_source(pe, s, it, key)
                    src = SOURCE[key][s]
                for c in range(DC):
                    transpose_tiles(s, it, f"xT {key}", c, src, c)

            def project(s, it, key, half, weights, columns):
                for t in tiles(half):
                    u = Use(s, it, key, t)
                    pe.wait_ge(u.evacuated, u.turn)
                    for c in range(DC):
                        last = pe.matmul(u.bank[:, 0:columns], XT[s][:, c, t * P:(t + 1) * P], weights[:, c, 0:columns],
                                         start=(c == 0), stop=(c == DC - 1))
                    last.then_inc(u.filled, 1)

            def project_v(half):
                def stage(s, it, key):
                    if half == 0:
                        for c in range(DC):
                            u = Use(s, it, f"xT {key}", c)
                            pe.wait_ge(u.evacuated, u.turn + 1)
                    if key == "L3":
                        project(s, it, "v L3", half, wv_sb, D)
                    else:
                        project(s, it, f"v {key}", half, w0_sb if key == "L0" else wg_sb, DA)
                return stage

            def scores_of_x(s, it, key):
                for c in range(DC):
                    u = Use(s, it, f"xT {key}", c)
                    pe.wait_ge(u.evacuated, u.turn + 1)
                u = Use(s, it, f"s {key}")
                pe.wait_ge(u.evacuated, u.turn)
                for t in range(NT):
                    for c in range(DC):
                        last = pe.matmul(u.bank[:, 2 * t:2 * t + 2], XT[s][:, c, t * P:(t + 1) * P],
                                         aw_sb[:, L1K.index(key), c, :], start=(c == 0), stop=(c == DC - 1))
                last.then_inc(u.filled, 1)

            def broadcast(s, it, key):
                if key in L1K:
                    u = Use(s, it, f"s {key}")
                    pe.wait_ge(u.evacuated, u.turn + 1)
                else:
                    for t in range(NT - 2, NT):
                        u = Use(s, it, f"v {key}", t)
                        pe.wait_ge(u.evacuated, u.turn + 1)
                u = Use(s, it, f"bc {key}")
                pe.wait_ge(u.evacuated, u.turn)
                for t in range(NT):
                    col = s12[s][:, t, 1:2] if key in L1K else V[s][:, t, D + 1:D + 2]
                    last = pe.transpose(u.bank[:, t * P:(t + 1) * P], col.broadcast_to([P, P]), ident[:])
                last.then_inc(u.filled, 1)

            def weights_transposed(half):
                def stage(s, it, key):
                    src = weights(s, key)
                    for t in tiles(half):
                        if key == "L2":
                            if t == 0:
                                pe.wait_ge(kept.sems[s], kept.value(it, key, NT - 1))
                        else:
                            pe.wait_ge(exp_done.sems[s], exp_done.value(it, key, t))
                        u = Use(s, it, f"pT {key}", t)
                        pe.wait_ge(u.evacuated, u.turn)
                        for j in range(NT):
                            last = pe.transpose(u.bank[:, j * P:(j + 1) * P], src[:, t, j * P:(j + 1) * P], ident[:])
                        last.then_inc(u.filled, 1)
                return stage

            def agg(s, it, key):
                pe.wait_ge(acc_evacuated.sems[s], acc_evacuated.value(it, key) - 1)
                src = SOURCE[key] if key in L1K else V
                if key in L1K[1:]:
                    wait_source(pe, s, it, key)
                for t in range(NT):
                    u = Use(s, it, f"pT {key}", t)
                    pe.wait_ge(u.evacuated, u.turn + 1)
                    for j in range(NT):
                        last = pe.matmul(acc[s][t // 2][:, t % 2, :], PT[s][:, j, t * P:(t + 1) * P], src[s][:, j, 0:D],
                                         start=(j == 0 and t % 2 == 0), stop=(j == NT - 1), skip_group_check=True)
                    if t % 2:
                        last.then_inc(acc_filled.sems[s], 1)

            def h_transposed(s, it, key):
                pe.wait_ge(normed.sems[s], normed.value(it, key + " h"))
                for c in range(DC):
                    transpose_tiles(s, it, f"hT {key}", c, HX[s], c)

            def ffn1(quarter):
                def stage(s, it, key):
                    l = L1K.index(key)
                    for c in range(DC):
                        u = Use(s, it, f"hT {key}", c)
                        pe.wait_ge(u.evacuated, u.turn + 1)
                    for f in range(quarter * FC // 4, (quarter + 1) * FC // 4):
                        u = Use(s, it, f"g {key}", f)
                        pe.wait_ge(u.evacuated, u.turn)
                        for c in range(DC):
                            last = pe.matmul(u.bank[:], w1_sb[:, l, c, f * P:(f + 1) * P], XT[s][:, c, :],
                                             start=(c == 0), stop=(c == DC - 1))
                        last.then_inc(u.filled, 1)
                return stage

            def ffn2(quarter):
                def stage(s, it, key):
                    l = L1K.index(key)
                    if quarter == 0:
                        pe.wait_ge(acc_evacuated.sems[s], acc_evacuated.value(it, key + " ffn") - 1)
                    for f in range(quarter * FC // 4, (quarter + 1) * FC // 4):
                        u = Use(s, it, f"g {key}", f)
                        pe.wait_ge(u.evacuated, u.turn + 1)
                    for t in range(NT):
                        for f in range(quarter * FC // 4, (quarter + 1) * FC // 4):
                            last = pe.matmul(acc[s][t // 2][:, t % 2, :], gT[:, f % (FC // 2), t * P:(t + 1) * P],
                                             w2_sb[:, l, f, :], start=(f == 0 and t % 2 == 0), stop=(f == FC - 1),
                                             skip_group_check=True)
                        if quarter == 3 and t % 2:
                            last.then_inc(acc_filled.sems[s], 1)
                return stage

            def project_transposed(name, w):
                def stage(s, it, key):
                    for m in range(DC):
                        u = Use(s, it, f"{name} L3", m)
                        pe.wait_ge(u.evacuated, u.turn)
                        for c in range(DC):
                            last = pe.matmul(u.bank[:], w[:, c, m * P:(m + 1) * P], XT[s][:, c, :],
                                             start=(c == 0), stop=(c == DC - 1))
                        last.then_inc(u.filled, 1)
                return stage

            def head_scores(half):
                def stage(s, it, key):
                    h = HEADS.index(key)
                    if half == 0:
                        pe.wait_ge(stacked[h % 2].sems[s], stacked[h % 2].value(it, key, 8 * 16 - 1))
                    for t in tiles(half):
                        u = Use(s, it, f"scores {key}", t)
                        pe.wait_ge(u.evacuated, u.turn)
                        pe.matmul(u.bank[:], q4[:, h % 2, t * P:(t + 1) * P], k4[:, h % 2, :],
                                  start=True, stop=True).then_inc(u.filled, 1)
                return stage

            def head_outputs(s, it, key):
                h = HEADS.index(key)
                if h == 1:
                    pe.wait_ge(acc_evacuated.sems[s], acc_evacuated.value(it, "heads") - 1)
                for t in range(NT - 2, NT):
                    u = Use(s, it, f"pT {key}", t)
                    pe.wait_ge(u.evacuated, u.turn + 1)
                for j in range(NT):
                    for hh in (h - 1, h):
                        m, r = hh // HPC, hh % HPC * DK
                        last = pe.matmul(flat(acc[s][m])[r:r + DK, :], V[s][:, j, hh * DK:(hh + 1) * DK], PT2[:, hh % 2, j, :],
                                         start=(j == 0), stop=(j == NT - 1), skip_group_check=True)
                if h == NH - 1:
                    last.then_inc(acc_filled.sems[s], 1)

            def heads_rden(s, it, key):
                pe.wait_ge(rden_ready.sems[s], rden_ready.value(it, "L3"))
                for i in range(2):
                    u = Use(s, it, "rdenT L3", i)
                    pe.wait_ge(u.evacuated, u.turn)
                    for t in range(NT // 2):
                        last = pe.transpose(u.bank[0:NH, t * P:(t + 1) * P], rden3[s][:, i * NT // 2 + t, :], ident[:])
                    last.then_inc(u.filled, 1)
                for i in range(2):
                    u = Use(s, it, "rdenT L3", i)
                    pe.wait_ge(u.evacuated, u.turn + 1)
                for m in range(DC):
                    u = Use(s, it, "rden L3", m)
                    pe.matmul(u.bank[:], head_rows[:, m, :], T[s][0:NH, 0, :], start=True, stop=True).then_inc(u.filled, 1)

            def proj(s, it, key):
                pe.wait_ge(acc_evacuated.sems[s], acc_evacuated.value(it, "L3") - 1)
                for t in range(NT):
                    for c in range(DC):
                        last = pe.matmul(acc[s][t // 2][:, t % 2, :], XT[s][:, c, t * P:(t + 1) * P], wo_sb[:, c, :],
                                         start=(c == 0 and t % 2 == 0), stop=(c == DC - 1), skip_group_check=True)
                    if t % 2:
                        last.then_inc(acc_filled.sems[s], 1)

            stages = {"xT": xT, "v1": project_v(0), "v2": project_v(1), "s": scores_of_x, "bc": broadcast, "pT1": weights_transposed(0),
                      "pT2": weights_transposed(1), "agg": agg,
                      "hT": h_transposed, "ffn1a": ffn1(0), "ffn1b": ffn1(1), "ffn1c": ffn1(2), "ffn1d": ffn1(3),
                      "ffn2a": ffn2(0), "ffn2b": ffn2(1), "ffn2c": ffn2(2), "ffn2d": ffn2(3),
                      "q": project_transposed("q", wq_sb), "k": project_transposed("k", wk_sb),
                      "scores1": head_scores(0), "scores2": head_scores(1), "pv": head_outputs, "heads": heads_rden, "proj": proj}
            walk(0, opening, stages)
            with pe.Fori(0, PAIRS - 1) as it:
                walk(it, to_a, stages)
                walk(it + 1, to_b, stages)
            walk(PAIRS - 1, closing, stages)


_INS = ["x", "adj", "L0_gnn_w", "L0_gnn_a1", "L0_gnn_a2", "L1_gnn_attn_w", "L1_gnn_attn_b", "L1_gnn_W1",
        "L1_gnn_b1", "L1_gnn_W2", "L1_gnn_b2", "L1_gnn_g1", "L1_gnn_beta1", "L1_gnn_g2", "L1_gnn_beta2",
        "L2_gnn_W", "L2_gnn_a", "L3_gnn_Wq", "L3_gnn_Wk", "L3_gnn_Wv", "L3_gnn_Wo"]


def kernel(**inputs):
    import numpy as np
    import concourse.bacc as bacc
    from concourse.bass_utils import run_bass_kernel_spmd as run

    nc = bacc.Bacc("TRN2", target_bir_lowering=False, num_devices=1)
    arrays, args = {}, []
    for name in _INS:
        a = np.ascontiguousarray(inputs[name])
        arrays[f"in_{name}"] = a
        args.append(nc.dram_tensor(f"in_{name}", a.shape, mybir.dt.from_np(a.dtype), kind="ExternalInput").ap())
    out = nc.dram_tensor("out", arrays["in_x"].shape, F32, kind="ExternalOutput").ap()
    build(nc, *args, out)
    r = run(nc, [arrays], core_ids=[0])
    return r.results[0]["out"]
```
